# Optimizing a Trainium2 kernel written in Bass

```python
import numpy as np
import jax
import jax.numpy as jnp

def _softmax(x, axis=-1):
    return jax.nn.softmax(x, axis=axis)

def _gelu(x):
    return jax.nn.gelu(x, approximate=True)

def _silu(x):
    return jax.nn.silu(x)

def _sigmoid(x):
    return jax.nn.sigmoid(x)

def _layernorm(x, axis=-1, eps=1e-05):
    m = jnp.mean(x, axis=axis, keepdims=True)
    v = jnp.var(x, axis=axis, keepdims=True)
    return (x - m) / jnp.sqrt(v + eps)

def _scatter_add(tgt, idx, src, axis=0):
    return tgt.at[idx].add(src)

def _segment_sum(src, seg, n):
    return jax.ops.segment_sum(src, seg, n)
kernel_name = 'mk_prb_d1_jaxref_r8_a2012c'

def setup_inputs(seed: int=0):
    np.random.seed(seed)
    _w = jnp.asarray

    def _L0_attn_setup():
        import jax, jax.numpy as jnp
        import numpy as np
        NUM_HEADS = 16
        EPS = 1e-06

        def _phi(x):
            return jax.nn.elu(x) + 1.0
        key = jax.random.key(seed)
        ks = jax.random.split(key, 5)
        B, L, D = (4, 1024, 128)
        scale = 0.02
        return {'x': jax.random.normal(ks[0], (B, L, D), dtype=jnp.float32), 'Wq': jax.random.normal(ks[1], (D, D), dtype=jnp.float32) * scale, 'Wk': jax.random.normal(ks[2], (D, D), dtype=jnp.float32) * scale, 'Wv': jax.random.normal(ks[3], (D, D), dtype=jnp.float32) * scale, 'Wo': jax.random.normal(ks[4], (D, D), dtype=jnp.float32) * scale}
    _L0_attn_in = _L0_attn_setup()

    def _L0_ffn_setup():
        import jax, jax.numpy as jnp
        import numpy as np
        B, S, D, H, O, E, K = (4, 256, 128, 256, 128, 8, 2)
        key = jax.random.key(seed)
        ks = jax.random.split(key, 8)
        x = jax.random.normal(ks[0], (B, S, D), dtype=jnp.float32)
        gate_w = jax.random.uniform(ks[1], (E, D), dtype=jnp.float32, minval=-1, maxval=1) * np.sqrt(6.0 / D)
        gate_b = jnp.zeros((E,), dtype=jnp.float32)
        w1 = jax.random.uniform(ks[2], (E, D, H), dtype=jnp.float32, minval=-1, maxval=1) * np.sqrt(6.0 / D)
        b1 = jnp.zeros((E, H), dtype=jnp.float32)
        w2 = jax.random.uniform(ks[3], (E, H, O), dtype=jnp.float32, minval=-1, maxval=1) * np.sqrt(6.0 / H)
        b2 = jnp.zeros((E, O), dtype=jnp.float32)
        return {'x': x, 'gate_w': gate_w, 'gate_b': gate_b, 'w1': w1, 'b1': b1, 'w2': w2, 'b2': b2}
    _L0_ffn_in = _L0_ffn_setup()
    _d = {'L0_attn_x': _L0_attn_in['x'], 'L0_attn_Wq': _L0_attn_in['Wq'], 'L0_attn_Wk': _L0_attn_in['Wk'], 'L0_attn_Wv': _L0_attn_in['Wv'], 'L0_attn_Wo': _L0_attn_in['Wo'], 'L0_ffn_gate_w': _L0_ffn_in['gate_w'], 'L0_ffn_gate_b': _L0_ffn_in['gate_b'], 'L0_ffn_w1': _L0_ffn_in['w1'], 'L0_ffn_b1': _L0_ffn_in['b1'], 'L0_ffn_w2': _L0_ffn_in['w2'], 'L0_ffn_b2': _L0_ffn_in['b2']}
    _x0 = _d['L0_attn_x']
    _d['L0_attn_x'] = jax.random.normal(jax.random.fold_in(jax.random.key(seed), 1), (8, 256, 128), dtype=_x0.dtype)
    del _x0
    return _d

def reference(L0_attn_x, L0_attn_Wq, L0_attn_Wk, L0_attn_Wv, L0_attn_Wo, L0_ffn_gate_w, L0_ffn_gate_b, L0_ffn_w1, L0_ffn_b1, L0_ffn_w2, L0_ffn_b2):

    def _L0_attn_ref(x, Wq, Wk, Wv, Wo):
        import jax, jax.numpy as jnp
        import numpy as np
        NUM_HEADS = 16
        EPS = 1e-06

        def _phi(x):
            return jax.nn.elu(x) + 1.0
        B, L, D = x.shape
        H = NUM_HEADS
        dh = D // H
        Q = x @ Wq
        K = x @ Wk
        V = x @ Wv
        Qh = Q.reshape(B, L, H, dh).transpose(0, 2, 1, 3)
        Kh = K.reshape(B, L, H, dh).transpose(0, 2, 1, 3)
        Vh = V.reshape(B, L, H, dh).transpose(0, 2, 1, 3)
        Qf = _phi(Qh)
        Kf = _phi(Kh)
        Kv = jnp.einsum('bhlm,bhln->bhmn', Kf, Vh)
        K1 = jnp.sum(Kf, axis=2)
        num = jnp.einsum('bhlm,bhmn->bhln', Qf, Kv)
        den = jnp.einsum('bhlm,bhm->bhl', Qf, K1) + EPS
        out = num / den[..., None]
        out = out.transpose(0, 2, 1, 3).reshape(B, L, D)
        return out @ Wo

    def _L0_ffn_ref(x, gate_w, gate_b, w1, b1, w2, b2):
        import jax, jax.numpy as jnp
        import numpy as np
        B, S, D, H, O, E, K = (4, 256, 128, 256, 128, 8, 2)
        logits = jnp.einsum('bsd,ed->bse', x, gate_w) + gate_b
        probs = jax.nn.softmax(logits, axis=-1)
        topk_vals, topk_idx = jax.lax.top_k(probs, K)
        h = jax.nn.relu(jnp.einsum('bsd,edh->bseh', x, w1) + b1)
        expert_out = jnp.einsum('bseh,eho->bseo', h, w2) + b2
        sel = jnp.take_along_axis(expert_out, topk_idx[..., None], axis=2)
        return jnp.sum(sel * topk_vals[..., None], axis=2)
    x = L0_attn_x
    xn = _layernorm(x, axis=-1)
    x = x + _L0_attn_ref(xn, L0_attn_Wq, L0_attn_Wk, L0_attn_Wv, L0_attn_Wo) + _L0_ffn_ref(xn, L0_ffn_gate_w, L0_ffn_gate_b, L0_ffn_w1, L0_ffn_b1, L0_ffn_w2, L0_ffn_b2)
    return x

_drawn_inputs = setup_inputs


def setup_inputs(seed=0):
    import zlib

    import numpy as np

    out = dict(_drawn_inputs(seed))
    spreads = {'L0_ffn_gate_b': (0.0, 0.1), 'L0_ffn_b1': (0.0, 0.1), 'L0_ffn_b2': (0.0, 0.1)}
    factors = {'L0_attn_Wq': 8.0, 'L0_attn_Wk': 8.0, 'L0_attn_Wv': 8.0, 'L0_attn_Wo': 8.0}
    for name, (base, spread) in spreads.items():
        noise = np.random.default_rng([zlib.crc32(name.encode()), seed]).standard_normal(out[name].shape)
        drawn = base * np.exp(spread * noise) if base else spread * noise
        out[name] = jnp.asarray(drawn.astype(out[name].dtype))
    for name, factor in factors.items():
        out[name] = (out[name] * factor).astype(out[name].dtype)
    return out
```

```python
from contextlib import ExitStack

import numpy as np

import concourse.bass as bass
from concourse import mybir

F32 = mybir.dt.float32
F32R = mybir.dt.float32r
U32 = mybir.dt.uint32
ALU = mybir.AluOpType
ACT = mybir.ActivationFunctionType
AX_X = mybir.AxisListType.X

P = 128
HEADS = 16
TOP = 2
LN_EPS = 1e-5
DEN_EPS = 1e-6


def shape_constants(D):
    rows = np.arange(D)
    head = rows // (D // HEADS)
    ident = np.eye(D, dtype=np.float32)
    same_head = (head[:, None] == head[None, :]).astype(np.float32)
    of_head = (head[:, None] == np.arange(HEADS)[None, :]).astype(np.float32)
    ramp = np.broadcast_to(np.arange(8, dtype=np.float32), (D, 8))
    return np.ascontiguousarray(np.concatenate([ident, same_head, of_head, ramp], axis=1))


def linear_attention_with_top2_experts(nc, x, wkvg, wq, wo, gate_b, w1, b1, w2, b2, consts, gates_dram, out):
    B, S, D = x.shape
    E, _, H = w1.shape
    T = B * S // P
    NBLK = T // 4
    BW = 4 * P
    R = S // P
    KC = H // P
    KVG = 2 * D + E
    NV = D + HEADS
    UNITS = E * NBLK
    PAIRS = E // 2
    UPP = 2 * NBLK
    assert D == P and R == 2 and KC == 2 and NBLK == 4 and E == 8

    x_view = x.rearrange("b (p r) d -> p b r d", r=R)
    out_view = out.rearrange("b (p r) d -> p b r d", r=R)
    w1_rows = w1.rearrange("e d h -> (e d) h")
    w2_view = w2.rearrange("e (c p) o -> p (e c) o", p=P)

    with ExitStack() as ctx:
        def sb(name, shape, dt=F32):
            return ctx.enter_context(nc.sbuf_tensor(name, shape, dt))

        def sem(name):
            return ctx.enter_context(nc.semaphore(name))

        x_tok = sb("x_tok", [P, T, D])
        xn = sb("xn", [P, T, D])
        x_hi = sb("x_hi", [P, T * P], F32R)
        x_lo = sb("x_lo", [P, T * P], F32R)
        cst = sb("cst", [P, D + NV + 8])
        wkvg_f = sb("wkvg_f", [P, KVG])
        wkvg_hi = sb("wkvg_hi", [P, KVG], F32R)
        wkvg_lo = sb("wkvg_lo", [P, KVG], F32R)
        wq_f = sb("wq_f", [P, D])
        wq_hi = sb("wq_hi", [P, D], F32R)
        wq_lo = sb("wq_lo", [P, D], F32R)
        wo_f = sb("wo_f", [P, D])
        gate_bias = sb("gate_bias", [P, E])
        b2_f = sb("b2_f", [P, E])
        w1_f = [sb(f"w1_f{i}", [P, H]) for i in range(2)]
        w2_f = [sb(f"w2_f{i}", [P, KC * D]) for i in range(2)]
        b1_f = [sb(f"b1_f{i}", [P, KC]) for i in range(2)]
        w1_hi = [sb(f"w1_hi{i}", [P, H], F32R) for i in range(2)]
        w1_lo = [sb(f"w1_lo{i}", [P, H], F32R) for i in range(2)]
        w2_hi = [sb(f"w2_hi{i}", [P, KC * D], F32R) for i in range(2)]
        w2_lo = [sb(f"w2_lo{i}", [P, KC * D], F32R) for i in range(2)]
        stats = sb("stats", [P, T, 6])
        mean_var = sb("mean_var", [P, T, 2])
        eps = sb("eps", [P, 1])
        ones = sb("ones", [P, H])
        std = sb("std", [P, T])
        rstd = sb("rstd", [P, T])
        qf = sb("qf", [P, T * P])
        kf = sb("kf", [P, T, D])
        vext = sb("vext", [P, T, NV])
        kv = sb("kv", [P, B, NV])
        den = sb("den", [P, T, HEADS])
        rden = sb("rden", [P, T, HEADS])
        att = sb("att", [P, T, D])
        attT = sb("attT", [P, T * P])
        logits = sb("logits", [P, T, E])
        top8 = sb("top8", [P, T, 8])
        idx8 = sb("idx8", [P, T, 8], U32)
        idxf = sb("idxf", [P, T, 8])
        shifted = sb("shifted", [P, T, E])
        expd = sb("expd", [P, T, E])
        expsum = sb("expsum", [P, T])
        rexpsum = sb("rexpsum", [P, T])
        is_first = sb("is_first", [P, T, E])
        is_second = sb("is_second", [P, T, E])
        picked = sb("picked", [P, T, E])
        gated = sb("gated", [P, T, E])
        gates = sb("gates", [P, E, T])
        gatesT = sb("gatesT", [P, P])
        gate_row = [sb(f"gate_row{i}", [P, T * P]) for i in range(2)]
        h_hi = [sb(f"h_hi{i}", [P, KC, BW], F32R) for i in range(2)]
        h_lo = [sb(f"h_lo{i}", [P, KC, BW], F32R) for i in range(2)]
        y = [sb(f"y{i}", [P, BW]) for i in range(4)]
        acc = sb("acc", [P, T * P])
        res = sb("res", [P, T, D])

        ident = cst[:, 0:D]
        kv_mask = cst[:, D:D + NV]
        ramp = cst[:, D + NV:D + NV + 8]

        banks = ctx.enter_context(nc.psum_tensor("banks", [P, 8, 512], F32))
        xT_ps = banks[:, 0, :]
        q_ps = banks[:, 1, :]
        kvg_ps = [banks[:, 2:4, :], banks[:, 4:6, :]]
        att_ps = banks[:, 6, :]
        num_ps = banks[:, 7, :]
        h_ps = [banks[:, 0:2, :], banks[:, 2:4, :]]
        y_ps = [banks[:, 4, :], banks[:, 5, :]]
        fin_ps = [banks[:, 6, :], banks[:, 7, :]]

        x_in = [sem(f"x_in{k}") for k in range(NBLK)]
        consts_in = sem("consts_in")
        gate_b_in = sem("gate_b_in")
        b1_in = [sem(f"b1_in{i}") for i in range(2)]
        b2_in = sem("b2_in")
        wkvg_in = sem("wkvg_in")
        wq_in = sem("wq_in")
        wo_in = sem("wo_in")
        w1_in = [sem(f"w1_in{i}") for i in range(2)]
        w2_in = [sem(f"w2_in{i}") for i in range(2)]
        eps_set = sem("eps_set")
        ones_set = sem("ones_set")
        stats_done = sem("stats_done")
        meanvar_done = sem("meanvar_done")
        std_done = sem("std_done")
        rstd_done = sem("rstd_done")
        xn_done = sem("xn_done")
        xT_done = sem("xT_done")
        xhi_done = sem("xhi_done")
        xlo_done = sem("xlo_done")
        wkvg_hi_done = sem("wkvg_hi_done")
        wkvg_split = sem("wkvg_split")
        wq_hi_done = sem("wq_hi_done")
        wq_split = sem("wq_split")
        w1_hi_done = sem("w1_hi_done")
        w1_split = sem("w1_split")
        w2_hi_done = sem("w2_hi_done")
        w2_split = sem("w2_split")
        q_done = sem("q_done")
        qneg_done = sem("qneg_done")
        qexp_done = sem("qexp_done")
        qf_done = sem("qf_done")
        kvg_done = sem("kvg_done")
        kneg_done = sem("kneg_done")
        kexp_done = sem("kexp_done")
        v_done = sem("v_done")
        kf_done = sem("kf_done")
        logits_done = sem("logits_done")
        kv_done = sem("kv_done")
        kvmask_done = sem("kvmask_done")
        num_done = sem("num_done")
        den_done = sem("den_done")
        rden_done = sem("rden_done")
        att_done = sem("att_done")
        attT_done = sem("attT_done")
        attT_copied = sem("attT_copied")
        wo_done = sem("wo_done")
        residual_done = sem("residual_done")
        top_done = sem("top_done")
        idx_done = sem("idx_done")
        gate_step = sem("gate_step")
        exp_done = sem("exp_done")
        gates_done = sem("gates_done")
        gatesT_done = sem("gatesT_done")
        gatesT_copied = sem("gatesT_copied")
        gates_out = sem("gates_out")
        gate_row_in = [sem(f"gate_row_in{i}") for i in range(2)]
        l1_done = sem("l1_done")
        relu_done = sem("relu_done")
        hhi_done = sem("hhi_done")
        hlo_done = sem("hlo_done")
        l2_done = sem("l2_done")
        gated_done = sem("gated_done")
        acc_done = sem("acc_done")
        fin_done = sem("fin_done")
        res_done = sem("res_done")
        out_written = sem("out_written")

        block = ctx.enter_context(nc.Block())

        def blk_cols(k):
            return slice(k * BW, (k + 1) * BW)

        def past(u, first):
            return not isinstance(u, int) or u >= first

        @block.sync
        def _(sp):
            for k in range(NBLK):
                sp.dma_start(x_tok[:, 4 * k:4 * k + 4, :].rearrange("p (b r) d -> p b r d", r=R),
                             x_view[:, 2 * k:2 * k + 2]).then_inc(x_in[k], 16)
            sp.dma_start(wo_f[:], wo).then_inc(wo_in, 16)

            def load_weights(e, par):
                sp.dma_start(w1_f[par][:], w1_rows[bass.ds(e * D, D), :]).then_inc(w1_in[par], 16)
                sp.dma_start(w2_f[par][:].rearrange("p (c o) -> p c o", c=KC), w2_view[:, bass.ds(e * KC, KC), :]
                             ).then_inc(w2_in[par], 16)

            def load_bias(e, par):
                sp.dma_start(b1_f[par][:], b1[bass.ds(e * P, P), :]).then_inc(b1_in[par], 16)

            for e in range(2):
                load_weights(e, e)
                load_bias(e, e)
            sp.wait_ge(gatesT_copied, 1)
            sp.dma_start(gates_dram, gatesT[:]).then_inc(gates_out, 16)
            sp.wait_ge(gates_out, 16)

            def load_gate_row(e, par):
                sp.dma_start(gate_row[par][:].rearrange("p (t c) -> p t c", c=P),
                             gates_dram[bass.ds(e * T, T), :].partition_broadcast(P)
                             ).then_inc(gate_row_in[par], 16)

            load_gate_row(0, 0)
            load_gate_row(1, 1)
            with sp.Fori(1, PAIRS) as p:
                for par in range(2):
                    sp.wait_ge(w2_split, 2 * p + par - 1)
                    load_weights(2 * p + par, par)
                    sp.wait_ge(gated_done, (2 * p + par - 1) * NBLK)
                    load_bias(2 * p + par, par)
                    load_gate_row(2 * p + par, par)
            for k in range(NBLK):
                sp.wait_ge(res_done, k + 1)
                sp.dma_start(out_view[:, 2 * k:2 * k + 2],
                             res[:, 4 * k:4 * k + 4, :].rearrange("p (b r) d -> p b r d", r=R)
                             ).then_inc(out_written, 16)
            sp.wait_ge(out_written, 16 * NBLK)

        @block.gpsimd
        def _(pool):
            nc.gpsimd.memset(eps[:], LN_EPS).then_inc(eps_set, 1)
            nc.gpsimd.memset(ones[:], 1.0).then_inc(ones_set, 1)
            nc.gpsimd.memset(vext[:, :, D:NV], 1.0).then_inc(ones_set, 1)

            def split_weights(e, par, rounds):
                for f, hi, lo, arrived, hi_done, split in (
                        (w1_f[par], w1_hi[par], w1_lo[par], w1_in[par], w1_hi_done, w1_split),
                        (w2_f[par], w2_hi[par], w2_lo[par], w2_in[par], w2_hi_done, w2_split)):
                    pool.wait_ge(arrived, 16 * rounds)
                    nc.gpsimd.tensor_tensor(hi[:], f[:], ones[:], ALU.mult).then_inc(hi_done, 1)
                    pool.wait_ge(hi_done, e + 1)
                    nc.gpsimd.tensor_tensor(lo[:], f[:], hi[:].bitcast(F32), ALU.subtract).then_inc(split, 1)

            def accumulate(u, j):
                pool.wait_ge(gated_done, u + 1)
                if past(u, 2 * NBLK):
                    pool.wait_ge(acc_done, u - 2 * NBLK + 1)
                cols = acc[:, blk_cols(j % NBLK)]
                nc.gpsimd.tensor_tensor(cols, cols, y[j % 4][:], ALU.add).then_inc(acc_done, 1)

            pool.wait_ge(ones_set, 2)
            split_weights(0, 0, 1)
            split_weights(1, 1, 1)
            pool.wait_ge(l1_done, NBLK * KC)
            pool.wait_ge(l2_done, NBLK)
            split_weights(2, 0, 2)
            for u in range(NBLK, 2 * NBLK):
                accumulate(u, u)
            pool.wait_ge(l1_done, 2 * NBLK * KC)
            pool.wait_ge(l2_done, 2 * NBLK)
            split_weights(3, 1, 2)
            for u in range(2 * NBLK, 3 * NBLK):
                accumulate(u, u)
            with pool.Fori(2, PAIRS) as p:
                for par in range(2):
                    pool.wait_ge(l1_done, (2 * p + par - 1) * NBLK * KC)
                    pool.wait_ge(l2_done, (2 * p + par - 1) * NBLK)
                    split_weights(2 * p + par, par, p + 1)
                    for j in range(NBLK):
                        accumulate((2 * p + par - 1) * NBLK + j, j)
            for u in range(UNITS - NBLK, UNITS):
                accumulate(u, u)

        def act_relu_and_hi(act, u, j, rounds):
            i = j % 2
            if j % NBLK == 0:
                act.wait_ge(b1_in[j // NBLK % 2], 16 * rounds)
            for c in range(KC):
                act.wait_ge(l1_done, u * KC + c + 1)
                nc.scalar.activation(h_ps[i][:, c, :], h_ps[i][:, c, :], ACT.Relu,
                                     bias=b1_f[j // NBLK % 2][:, c:c + 1]).then_inc(relu_done, 1)
                act.wait_ge(relu_done, u * KC + c + 1)
                if past(u, 2):
                    act.wait_ge(l2_done, u - 1)
                nc.scalar.copy(h_hi[i][:, c, :], h_ps[i][:, c, :]).then_inc(hhi_done, 1)

        @block.scalar
        def _(act):
            act.dma_start(wkvg_f[:], wkvg).then_inc(wkvg_in, 16)
            act.dma_start(cst[:], consts).then_inc(consts_in, 16)
            act.dma_start(wq_f[:], wq).then_inc(wq_in, 16)
            act.dma_start(gate_bias[:], gate_b.partition_broadcast(P)).then_inc(gate_b_in, 16)
            act.dma_start(b2_f[:], b2).then_inc(b2_in, 16)
            act.wait_ge(eps_set, 1)
            for k in range(NBLK):
                act.wait_ge(meanvar_done, 4 * k + 4)
                nc.scalar.activation(std[:, 4 * k:4 * k + 4], mean_var[:, 4 * k:4 * k + 4, 1], ACT.Sqrt,
                                     bias=eps[:, 0:1]).then_inc(std_done, 1)
            for k in range(NBLK):
                act.wait_ge(xT_done, k + 1)
                nc.scalar.copy(x_hi[:, blk_cols(k)], xT_ps).then_inc(xhi_done, 1)
                for b in (2 * k, 2 * k + 1):
                    ts = slice(2 * b, 2 * b + 2)
                    act.wait_ge(kvg_done, b + 1)
                    nc.scalar.activation(kf[:, ts, :], kvg_ps[b % 2][:, :, 0:D], ACT.Relu, scale=-1.0
                                         ).then_inc(kneg_done, 1)
                    nc.scalar.copy(vext[:, ts, 0:D], kvg_ps[b % 2][:, :, D:2 * D]).then_inc(v_done, 1)
                    act.wait_ge(kneg_done, b + 1)
                    nc.scalar.activation(kf[:, ts, :], kf[:, ts, :], ACT.Exp, scale=-1.0).then_inc(kexp_done, 1)
                act.wait_ge(q_done, k + 1)
                nc.scalar.activation(qf[:, blk_cols(k)], q_ps, ACT.Relu, scale=-1.0).then_inc(qneg_done, 1)
                act.wait_ge(qneg_done, k + 1)
                nc.scalar.activation(qf[:, blk_cols(k)], qf[:, blk_cols(k)], ACT.Exp, scale=-1.0
                                     ).then_inc(qexp_done, 1)
            act.wait_ge(gate_step, 1)
            nc.scalar.activation(expd[:], shifted[:], ACT.Exp).then_inc(exp_done, 1)
            for u in range(UPP):
                if u % 2 == 0:
                    act.wait_ge(attT_done, u // 2 + 1)
                    nc.scalar.copy(attT[:, blk_cols(u // 2)], att_ps).then_inc(attT_copied, 1)
                act_relu_and_hi(act, u, u, 1)
            with act.Fori(1, PAIRS) as p:
                for j in range(UPP):
                    act_relu_and_hi(act, UPP * p + j, j, p + 1)

        def mask_kv(dve, k):
            dve.wait_ge(kv_done, k + 1)
            if k == 0:
                dve.wait_ge(consts_in, 16)
            nc.vector.tensor_tensor(kv[:, 2 * k:2 * k + 2, :],
                                    att_ps.rearrange("p (b n) -> p b n", b=2)[:, :, 0:NV],
                                    kv_mask.unsqueeze(1).to_broadcast([P, 2, NV]), ALU.mult
                                    ).then_inc(kvmask_done, 1)

        @block.vector
        def _(dve):
            for k in range(NBLK):
                dve.wait_ge(x_in[k], 16)
                for t in range(4 * k, 4 * k + 4):
                    nc.vector.bn_stats(stats[:, t, :], x_tok[:, t, :]).then_inc(stats_done, 1)
                for t in range(4 * k, 4 * k + 4):
                    dve.wait_ge(stats_done, t + 1)
                    nc.vector.bn_aggr(mean_var[:, t, :], stats[:, t, :]).then_inc(meanvar_done, 1)
            dve.wait_ge(wkvg_in, 16)
            nc.vector.tensor_copy(wkvg_hi[:], wkvg_f[:]).then_inc(wkvg_hi_done, 1)

            def normalise(k):
                dve.wait_ge(std_done, k + 1)
                nc.vector.reciprocal(rstd[:, 4 * k:4 * k + 4], std[:, 4 * k:4 * k + 4]).then_inc(rstd_done, 1)
                dve.wait_ge(rstd_done, k + 1)
                for t in range(4 * k, 4 * k + 4):
                    nc.vector.tensor_scalar(xn[:, t, :], x_tok[:, t, :], mean_var[:, t, 0:1], rstd[:, t:t + 1],
                                            ALU.subtract, ALU.mult).then_inc(xn_done, 1)

            def split_x(k):
                dve.wait_ge(xhi_done, k + 1)
                nc.vector.tensor_tensor(x_lo[:, blk_cols(k)], xT_ps, x_hi[:, blk_cols(k)].bitcast(F32),
                                        ALU.subtract).then_inc(xlo_done, 1)

            normalise(0)
            dve.wait_ge(wkvg_hi_done, 1)
            nc.vector.tensor_tensor(wkvg_lo[:], wkvg_f[:], wkvg_hi[:].bitcast(F32), ALU.subtract
                                    ).then_inc(wkvg_split, 1)
            dve.wait_ge(wq_in, 16)
            nc.vector.tensor_copy(wq_hi[:], wq_f[:]).then_inc(wq_hi_done, 1)
            split_x(0)
            normalise(1)
            dve.wait_ge(wq_hi_done, 1)
            nc.vector.tensor_tensor(wq_lo[:], wq_f[:], wq_hi[:].bitcast(F32), ALU.subtract).then_inc(wq_split, 1)
            dve.wait_ge(gate_b_in, 16)
            for k in range(NBLK):
                for b in (2 * k, 2 * k + 1):
                    ts = slice(2 * b, 2 * b + 2)
                    dve.wait_ge(kexp_done, b + 1)
                    dve.wait_ge(v_done, b + 1)
                    nc.vector.tensor_tensor(logits[:, ts, :], kvg_ps[b % 2][:, :, 2 * D:KVG],
                                            gate_bias[:].unsqueeze(1).to_broadcast([P, 2, E]), ALU.add
                                            ).then_inc(logits_done, 1)
                    nc.vector.scalar_tensor_tensor(out=kf[:, ts, :], in0=kvg_ps[b % 2][:, :, 0:D], scalar=0.0,
                                                   in1=kf[:, ts, :], op0=ALU.max, op1=ALU.add
                                                   ).then_inc(kf_done, 1)
                if k + 1 < NBLK:
                    split_x(k + 1)
                dve.wait_ge(qexp_done, k + 1)
                nc.vector.scalar_tensor_tensor(out=qf[:, blk_cols(k)], in0=q_ps, scalar=0.0,
                                               in1=qf[:, blk_cols(k)], op0=ALU.max, op1=ALU.add
                                               ).then_inc(qf_done, 1)
                if k + 2 < NBLK:
                    normalise(k + 2)
                if k >= 1:
                    mask_kv(dve, k - 1)
            dve.wait_ge(logits_done, B)
            for t in range(T):
                nc.vector.max(top8[:, t, :], logits[:, t, :]).then_inc(top_done, 1)
            dve.wait_ge(top_done, T)
            nc.vector.tensor_tensor(shifted[:], logits[:], top8[:, :, 0:1].to_broadcast([P, T, E]),
                                    ALU.subtract).then_inc(gate_step, 1)
            for t in range(T):
                nc.vector.max_index(idx8[:, t, :], top8[:, t, :], logits[:, t, :]).then_inc(idx_done, 1)
            mask_kv(dve, NBLK - 1)
            dve.wait_ge(idx_done, T)
            nc.vector.tensor_copy(idxf[:, :, 0:TOP], idx8[:, :, 0:TOP]).then_inc(gate_step, 1)
            dve.wait_ge(exp_done, 1)
            nc.vector.reduce_sum(expsum[:], expd[:], AX_X).then_inc(gate_step, 1)
            dve.wait_ge(gate_step, 2)
            all_ramp = ramp.unsqueeze(1).to_broadcast([P, T, E])
            dve.wait_ge(consts_in, 16)
            nc.vector.tensor_tensor(is_first[:], all_ramp, idxf[:, :, 0:1].to_broadcast([P, T, E]),
                                    ALU.is_equal).then_inc(gate_step, 1)
            nc.vector.tensor_tensor(is_second[:], all_ramp, idxf[:, :, 1:2].to_broadcast([P, T, E]),
                                    ALU.is_equal).then_inc(gate_step, 1)
            dve.wait_ge(gate_step, 3)
            nc.vector.reciprocal(rexpsum[:], expsum[:]).then_inc(gate_step, 1)
            dve.wait_ge(gate_step, 5)
            nc.vector.tensor_tensor(picked[:], is_first[:], is_second[:], ALU.add).then_inc(gate_step, 1)
            dve.wait_ge(gate_step, 6)
            nc.vector.tensor_tensor(gated[:], expd[:], rexpsum[:].unsqueeze(2).to_broadcast([P, T, E]),
                                    ALU.mult).then_inc(gate_step, 1)
            dve.wait_ge(gate_step, 8)
            nc.vector.tensor_tensor(gates[:].rearrange("p e t -> p t e"), gated[:], picked[:], ALU.mult
                                    ).then_inc(gates_done, 1)

            def divide(b):
                ts = slice(2 * b, 2 * b + 2)
                both = num_ps[:, 0:2 * NV].rearrange("p (r n) -> p r n", r=2)
                dve.wait_ge(num_done, b + 1)
                nc.vector.tensor_scalar(den[:, ts, :], both[:, :, D:NV], DEN_EPS, None, ALU.add
                                        ).then_inc(den_done, 1)
                dve.wait_ge(den_done, b + 1)
                nc.vector.reciprocal(rden[:, ts, :], den[:, ts, :]).then_inc(rden_done, 1)
                dve.wait_ge(rden_done, b + 1)
                for r in range(2):
                    t = 2 * b + r
                    last = nc.vector.tensor_tensor(
                        att[:, t, :].rearrange("p (h d) -> p h d", h=HEADS),
                        both[:, r, 0:D].rearrange("p (h d) -> p h d", h=HEADS),
                        rden[:, t, :].unsqueeze(2).to_broadcast([P, HEADS, D // HEADS]), ALU.mult)
                    last.then_inc(att_done, 1)

            def add_residual(k):
                dve.wait_ge(wo_done, k + 1)
                cols = x_tok[:, 4 * k:4 * k + 4, :]
                nc.vector.tensor_tensor(cols, cols, att_ps.rearrange("p (t d) -> p t d", t=4), ALU.add
                                        ).then_inc(residual_done, 1)

            def lo_of_h(u, j):
                i = j % 2
                for c in range(KC):
                    dve.wait_ge(hhi_done, u * KC + c + 1)
                    nc.vector.tensor_tensor(h_lo[i][:, c, :], h_ps[i][:, c, :], h_hi[i][:, c, :].bitcast(F32),
                                            ALU.subtract).then_inc(hlo_done, 1)

            def gate_output(u, j, e, rounds):
                blk = j % NBLK
                par = j // NBLK % 2
                dve.wait_ge(l2_done, u + 1)
                if blk == 0:
                    dve.wait_ge(gate_row_in[par], rounds * 16)
                first = isinstance(u, int) and u < NBLK
                if past(u, 2 * NBLK):
                    dve.wait_ge(acc_done, u - 2 * NBLK + 1)
                dst = acc[:, blk_cols(blk)] if first else y[j % 4][:]
                nc.vector.scalar_tensor_tensor(out=dst, in0=y_ps[j % 2], scalar=b2_f[:, bass.ds(e, 1)],
                                               in1=gate_row[par][:, blk_cols(blk)], op0=ALU.add, op1=ALU.mult
                                               ).then_inc(gated_done, 1)

            divide(0)
            divide(1)
            dve.wait_ge(gatesT_done, 1)
            nc.vector.tensor_copy(gatesT[:], att_ps[:, 0:P]).then_inc(gatesT_copied, 1)
            dve.wait_ge(b2_in, 16)
            for u in range(UPP):
                lo_of_h(u, u)
                if u % 2 == 1:
                    add_residual(u // 2)
                if u + 2 < B:
                    divide(u + 2)
                if u >= 1:
                    gate_output(u - 1, u - 1, (u - 1) // NBLK, 1)
            with dve.Fori(1, PAIRS) as p:
                for j in range(UPP):
                    lo_of_h(UPP * p + j, j)
                    if j == 0:
                        gate_output(UPP * p - 1, UPP - 1, 2 * p - 1, p)
                    else:
                        gate_output(UPP * p + (j - 1), j - 1, 2 * p + (j - 1) // NBLK, p + 1)
            gate_output(UNITS - 1, UPP - 1, E - 1, PAIRS)
            for k in range(NBLK):
                dve.wait_ge(fin_done, k + 1)
                nc.vector.tensor_tensor(res[:, 4 * k:4 * k + 4, :],
                                        fin_ps[k % 2].rearrange("p (t d) -> p t d", t=4),
                                        x_tok[:, 4 * k:4 * k + 4, :], ALU.add).then_inc(res_done, 1)

        @block.tensor
        def _(pe):
            def three(out_ap, lhs_hi, lhs_lo, rhs_hi, rhs_lo, start=True, stop=True):
                nc.tensor.matmul(out_ap, lhs_hi, rhs_hi, start=start, stop=False)
                nc.tensor.matmul(out_ap, lhs_hi, rhs_lo, start=False, stop=False)
                return nc.tensor.matmul(out_ap, lhs_lo, rhs_hi, start=False, stop=stop)

            def transpose_x(k):
                if k == 0:
                    pe.wait_ge(consts_in, 16)
                pe.wait_ge(xn_done, 4 * k + 4)
                if k >= 1:
                    pe.wait_ge(xlo_done, k)
                for t in range(4):
                    last = nc.tensor.transpose(xT_ps[:, t * P:(t + 1) * P], xn[:, 4 * k + t, :], ident)
                last.then_inc(xT_done, 1)

            def project_kvg(b):
                if b == 0:
                    pe.wait_ge(wkvg_split, 1)
                pe.wait_ge(xlo_done, b // 2 + 1)
                if b >= 2:
                    pe.wait_ge(kf_done, b - 1)
                for r in range(2):
                    cols = slice((2 * b + r) * P, (2 * b + r + 1) * P)
                    last = three(kvg_ps[b % 2][:, r, 0:KVG], x_hi[:, cols], x_lo[:, cols], wkvg_hi[:], wkvg_lo[:])
                last.then_inc(kvg_done, 1)

            def project_q(k):
                if k == 0:
                    pe.wait_ge(wq_split, 1)
                else:
                    pe.wait_ge(qf_done, k)
                three(q_ps, wq_hi[:], wq_lo[:], x_hi[:, blk_cols(k)], x_lo[:, blk_cols(k)]).then_inc(q_done, 1)

            def keys_values(k):
                pe.wait_ge(kf_done, 2 * k + 2)
                if k == 0:
                    pe.wait_ge(ones_set, 2)
                else:
                    pe.wait_ge(kvmask_done, k)
                for b in range(2):
                    for r in range(2):
                        t = 4 * k + 2 * b + r
                        last = nc.tensor.matmul(att_ps[:, 256 * b:256 * b + NV], kf[:, t, :], vext[:, t, :],
                                                start=(r == 0), stop=(r == 1))
                last.then_inc(kv_done, 1)

            def numerator(b):
                pe.wait_ge(qf_done, b // 2 + 1)
                pe.wait_ge(kvmask_done, b // 2 + 1)
                if b >= 1:
                    pe.wait_ge(att_done, 2 * b)
                for r in range(2):
                    t = 2 * b + r
                    last = nc.tensor.matmul(num_ps[:, r * NV:(r + 1) * NV], qf[:, t * P:(t + 1) * P], kv[:, b, :],
                                            start=True, stop=True)
                last.then_inc(num_done, 1)

            def transpose_att(k):
                pe.wait_ge(att_done, 4 * k + 4)
                if k >= 1:
                    pe.wait_ge(residual_done, k)
                for t in range(4):
                    last = nc.tensor.transpose(att_ps[:, t * P:(t + 1) * P], att[:, 4 * k + t, :], ident)
                last.then_inc(attT_done, 1)

            def project_out(k):
                if k == 0:
                    pe.wait_ge(wo_in, 16)
                pe.wait_ge(attT_copied, k + 1)
                for t in range(4):
                    last = nc.tensor.matmul(att_ps[:, t * P:(t + 1) * P], attT[:, (4 * k + t) * P:(4 * k + t + 1) * P],
                                            wo_f[:], start=True, stop=True)
                last.then_inc(wo_done, 1)

            def first_product(u, j, e):
                par, blk, i = j // NBLK % 2, j % NBLK, j % 2
                if blk == 0:
                    pe.wait_ge(w1_split, e + 1)
                if past(u, 2):
                    pe.wait_ge(hlo_done, (u - 1) * KC)
                for c in range(KC):
                    w = slice(c * P, (c + 1) * P)
                    three(h_ps[i][:, c, :], w1_hi[par][:, w], w1_lo[par][:, w],
                          x_hi[:, blk_cols(blk)], x_lo[:, blk_cols(blk)]).then_inc(l1_done, 1)

            def second_product(u, j, e):
                par, blk, i = j // NBLK % 2, j % NBLK, j % 2
                if blk == 0:
                    pe.wait_ge(w2_split, e + 1)
                if past(u, 2):
                    pe.wait_ge(gated_done, u - 1)
                for c in range(KC):
                    w = slice(c * D, (c + 1) * D)
                    pe.wait_ge(hlo_done, u * KC + c + 1)
                    last = three(y_ps[i], w2_hi[par][:, w], w2_lo[par][:, w], h_hi[i][:, c, :], h_lo[i][:, c, :],
                                 start=(c == 0), stop=(c == KC - 1))
                last.then_inc(l2_done, 1)

            for k in range(NBLK):
                transpose_x(k)
                project_kvg(2 * k)
                project_kvg(2 * k + 1)
                project_q(k)
                if k >= 1:
                    keys_values(k - 1)
            keys_values(NBLK - 1)
            numerator(0)
            numerator(1)
            pe.wait_ge(gates_done, 1)
            pe.wait_ge(kvmask_done, NBLK)
            nc.tensor.transpose(att_ps[:, 0:P], gates[:].rearrange("p e t -> p (e t)"), ident).then_inc(gatesT_done, 1)
            pe.wait_ge(qf_done, NBLK)
            pe.wait_ge(gatesT_copied, 1)
            for u in range(UPP):
                if u % 2 == 0:
                    transpose_att(u // 2)
                else:
                    project_out(u // 2)
                if u + 2 < B:
                    numerator(u + 2)
                first_product(u, u, u // NBLK)
                if u >= 1:
                    second_product(u - 1, u - 1, (u - 1) // NBLK)
            with pe.Fori(1, PAIRS) as p:
                for j in range(UPP):
                    first_product(UPP * p + j, j, 2 * p + j // NBLK)
                    if j == 0:
                        second_product(UPP * p - 1, UPP - 1, 2 * p - 1)
                    else:
                        second_product(UPP * p + (j - 1), j - 1, 2 * p + (j - 1) // NBLK)
            second_product(UNITS - 1, UPP - 1, E - 1)
            for k in range(NBLK):
                pe.wait_ge(acc_done, UNITS - 2 * NBLK + k + 1)
                if k >= 2:
                    pe.wait_ge(res_done, k - 1)
                for t in range(4):
                    last = nc.tensor.transpose(fin_ps[k % 2][:, t * P:(t + 1) * P],
                                               acc[:, (4 * k + t) * P:(4 * k + t + 1) * P], ident)
                last.then_inc(fin_done, 1)


def kernel(L0_attn_x, L0_attn_Wq, L0_attn_Wk, L0_attn_Wv, L0_attn_Wo, L0_ffn_gate_w, L0_ffn_gate_b,
           L0_ffn_w1, L0_ffn_b1, L0_ffn_w2, L0_ffn_b2):
    import concourse.bacc as bacc
    from concourse.bass_utils import run_bass_kernel_spmd

    x = np.ascontiguousarray(L0_attn_x)
    E, D, H = L0_ffn_w1.shape
    T = x.shape[0] * x.shape[1] // P
    arrays = {
        "x": x,
        "wkvg": np.ascontiguousarray(np.concatenate(
            [np.asarray(L0_attn_Wk), np.asarray(L0_attn_Wv), np.asarray(L0_ffn_gate_w).T], axis=1)),
        "wq": np.ascontiguousarray(L0_attn_Wq),
        "wo": np.ascontiguousarray(L0_attn_Wo),
        "gate_b": np.ascontiguousarray(L0_ffn_gate_b),
        "w1": np.ascontiguousarray(L0_ffn_w1),
        "b1": np.ascontiguousarray(np.asarray(L0_ffn_b1).reshape(E, H // P, P).transpose(0, 2, 1)).reshape(E * P, H // P),
        "w2": np.ascontiguousarray(L0_ffn_w2),
        "b2": np.ascontiguousarray(np.asarray(L0_ffn_b2).T),
        "consts": shape_constants(D),
    }
    nc = bacc.Bacc("TRN2", target_bir_lowering=False, num_devices=1)
    args = [nc.dram_tensor(f"in_{n}", a.shape, mybir.dt.from_np(a.dtype), kind="ExternalInput").ap()
            for n, a in arrays.items()]
    gates_dram = nc.dram_tensor("gates_dram", (E * T, P), F32, kind="Internal").ap()
    out = nc.dram_tensor("out", x.shape, F32, kind="ExternalOutput").ap()
    linear_attention_with_top2_experts(nc, *args, gates_dram, out)
    r = run_bass_kernel_spmd(nc, [{f"in_{n}": a for n, a in arrays.items()}], core_ids=[0])
    return np.asarray(r.results[0]["out"])
```

```python
from contextlib import ExitStack

import numpy as np

import concourse.bass as bass
from concourse import mybir

F32 = mybir.dt.float32
F32R = mybir.dt.float32r
U32 = mybir.dt.uint32
ALU = mybir.AluOpType
ACT = mybir.ActivationFunctionType
AX_X = mybir.AxisListType.X

P = 128
HEADS = 16
TOP = 2
LN_EPS = 1e-5
DEN_EPS = 1e-6


def shape_constants(D):
    rows = np.arange(D)
    head = rows // (D // HEADS)
    ident = np.eye(D, dtype=np.float32)
    same_head = (head[:, None] == head[None, :]).astype(np.float32)
    of_head = (head[:, None] == np.arange(HEADS)[None, :]).astype(np.float32)
    ramp = np.broadcast_to(np.arange(8, dtype=np.float32), (D, 8))
    return np.ascontiguousarray(np.concatenate([ident, same_head, of_head, ramp], axis=1))


def linear_attention_with_top2_experts(nc, x, wkvg, wq, wo, gate_b, w1, b1, w2, b2, consts, gates_dram, out):
    B, S, D = x.shape
    E, _, H = w1.shape
    T = B * S // P
    NBLK = T // 4
    BW = 4 * P
    R = S // P
    KC = H // P
    KVG = 2 * D + E
    NV = D + HEADS
    UNITS = E * NBLK
    PAIRS = E // 2
    UPP = 2 * NBLK
    WARM_UPS = 11
    assert D == P and R == 2 and KC == 2 and NBLK == 4 and E == 8

    x_view = x.rearrange("b (p r) d -> p b r d", r=R)
    out_view = out.rearrange("b (p r) d -> p b r d", r=R)
    w1_rows = w1.rearrange("e d h -> (e d) h")
    w2_view = w2.rearrange("e (c p) o -> p (e c) o", p=P)

    with ExitStack() as ctx:
        def sb(name, shape, dt=F32):
            return ctx.enter_context(nc.sbuf_tensor(name, shape, dt))

        def sem(name):
            return ctx.enter_context(nc.semaphore(name))

        x_tok = sb("x_tok", [P, T, D])
        xn = sb("xn", [P, T, D])
        x_hi = sb("x_hi", [P, T * P], F32R)
        x_lo = sb("x_lo", [P, T * P], F32R)
        cst = sb("cst", [P, D + NV + 8])
        wkvg_f = sb("wkvg_f", [P, KVG])
        wkvg_hi = sb("wkvg_hi", [P, KVG], F32R)
        wkvg_lo = sb("wkvg_lo", [P, KVG], F32R)
        wq_f = sb("wq_f", [P, D])
        wq_hi = sb("wq_hi", [P, D], F32R)
        wq_lo = sb("wq_lo", [P, D], F32R)
        wo_f = sb("wo_f", [P, D])
        gate_bias = sb("gate_bias", [P, E])
        b2_f = sb("b2_f", [P, E])
        w1_f = [sb(f"w1_f{i}", [P, H]) for i in range(2)]
        w2_f = [sb(f"w2_f{i}", [P, KC * D]) for i in range(2)]
        b1_f = [sb(f"b1_f{i}", [P, KC]) for i in range(2)]
        w1_hi = [sb(f"w1_hi{i}", [P, H], F32R) for i in range(2)]
        w1_lo = [sb(f"w1_lo{i}", [P, H], F32R) for i in range(2)]
        w2_hi = [sb(f"w2_hi{i}", [P, KC * D], F32R) for i in range(2)]
        w2_lo = [sb(f"w2_lo{i}", [P, KC * D], F32R) for i in range(2)]
        stats = sb("stats", [P, T, 6])
        mean_var = sb("mean_var", [P, T, 2])
        eps = sb("eps", [P, 1])
        ones = sb("ones", [P, KVG])
        warm = sb("warm", [P, 2])
        std = sb("std", [P, T])
        rstd = sb("rstd", [P, T])
        qf = sb("qf", [P, T * P])
        kf = sb("kf", [P, T, D])
        vext = sb("vext", [P, T, NV])
        kv = sb("kv", [P, B, NV])
        den = sb("den", [P, T, HEADS])
        rden = sb("rden", [P, T, HEADS])
        att = sb("att", [P, T, D])
        attT = sb("attT", [P, T * P])
        logits = sb("logits", [P, T, E])
        top8 = sb("top8", [P, T, 8])
        idx8 = sb("idx8", [P, T, 8], U32)
        idxf = sb("idxf", [P, T, 8])
        shifted = sb("shifted", [P, T, E])
        expd = sb("expd", [P, T, E])
        expsum = sb("expsum", [P, T])
        rexpsum = sb("rexpsum", [P, T])
        is_first = sb("is_first", [P, T, E])
        is_second = sb("is_second", [P, T, E])
        picked = sb("picked", [P, T, E])
        gates = sb("gates", [P, E, T])
        gatesT = sb("gatesT", [P, P])
        gate_row = [sb(f"gate_row{i}", [P, T * P]) for i in range(2)]
        h_hi = [sb(f"h_hi{i}", [P, KC, BW], F32R) for i in range(2)]
        h_lo = [sb(f"h_lo{i}", [P, KC, BW], F32R) for i in range(2)]
        y = [sb(f"y{i}", [P, BW]) for i in range(4)]
        acc = sb("acc", [P, T * P])
        res = sb("res", [P, T, D])

        ident = cst[:, 0:D]
        kv_mask = cst[:, D:D + NV]
        ramp = cst[:, D + NV:D + NV + 8]

        banks = ctx.enter_context(nc.psum_tensor("banks", [P, 8, 512], F32))
        xT_ps = [banks[:, 0, :], banks[:, 1, :]]
        q_ps = banks[:, 7, :]
        kvg_ps = [banks[:, 2:4, :], banks[:, 4:6, :]]
        att_ps = banks[:, 6, :]
        num_ps = banks[:, 7, :]
        h_ps = [banks[:, 0:2, :], banks[:, 2:4, :]]
        y_ps = [banks[:, 4, :], banks[:, 5, :]]
        gatesT_ps = banks[:, 5, 0:P]
        fin_ps = [banks[:, 6, :], banks[:, 7, :]]

        x_in = [sem(f"x_in{k}") for k in range(NBLK)]
        consts_in = sem("consts_in")
        gate_b_in = sem("gate_b_in")
        b1_in = [sem(f"b1_in{i}") for i in range(2)]
        b2_in = sem("b2_in")
        wkvg_in = sem("wkvg_in")
        wq_in = sem("wq_in")
        wo_in = sem("wo_in")
        w1_in = [sem(f"w1_in{i}") for i in range(2)]
        w2_in = [sem(f"w2_in{i}") for i in range(2)]
        eps_set = sem("eps_set")
        ones_set = sem("ones_set")
        stats_done = sem("stats_done")
        meanvar_done = sem("meanvar_done")
        std_done = sem("std_done")
        pe_warm = sem("pe_warm")
        warm_done = sem("warm_done")
        rstd_done = sem("rstd_done")
        xn_done = sem("xn_done")
        centred = sem("centred")
        xn_pool_done = sem("xn_pool_done")
        xT_done = sem("xT_done")
        xhi_done = sem("xhi_done")
        xlo_done = sem("xlo_done")
        wkvg_hi_done = sem("wkvg_hi_done")
        wkvg_split = sem("wkvg_split")
        wq_hi_done = sem("wq_hi_done")
        wq_split = sem("wq_split")
        w1_hi_done = sem("w1_hi_done")
        w1_split = sem("w1_split")
        w2_hi_done = sem("w2_hi_done")
        w2_split = sem("w2_split")
        q_done = sem("q_done")
        qneg_done = sem("qneg_done")
        qexp_done = sem("qexp_done")
        qf_done = sem("qf_done")
        kvg_done = sem("kvg_done")
        kneg_done = sem("kneg_done")
        kexp_done = sem("kexp_done")
        v_done = sem("v_done")
        kf_done = sem("kf_done")
        logits_done = sem("logits_done")
        kv_done = sem("kv_done")
        kvmask_done = sem("kvmask_done")
        num_done = sem("num_done")
        den_done = sem("den_done")
        rden_done = sem("rden_done")
        att_done = sem("att_done")
        attT_done = sem("attT_done")
        attT_copied = sem("attT_copied")
        wo_done = sem("wo_done")
        residual_done = sem("residual_done")
        top_done = sem("top_done")
        idx_done = sem("idx_done")
        gate_step = sem("gate_step")
        exp_done = sem("exp_done")
        gates_done = sem("gates_done")
        gatesT_done = sem("gatesT_done")
        gatesT_copied = sem("gatesT_copied")
        gates_out = sem("gates_out")
        gate_row_in = [sem(f"gate_row_in{i}") for i in range(2)]
        l1_done = sem("l1_done")
        relu_done = sem("relu_done")
        hhi_done = sem("hhi_done")
        hlo_done = sem("hlo_done")
        l2_done = sem("l2_done")
        gated_done = sem("gated_done")
        acc_done = sem("acc_done")
        last_acc_done = sem("last_acc_done")
        fin_done = sem("fin_done")
        res_done = sem("res_done")
        out_written = sem("out_written")

        block = ctx.enter_context(nc.Block())

        def blk_cols(k):
            return slice(k * BW, (k + 1) * BW)

        def past(u, first):
            return not isinstance(u, int) or u >= first

        @block.sync
        def _(sp):
            def load_x(k):
                sp.dma_start(x_tok[:, 4 * k:4 * k + 4, :].rearrange("p (b r) d -> p b r d", r=R),
                             x_view[:, 2 * k:2 * k + 2]).then_inc(x_in[k], 16)

            load_x(0)
            load_x(1)
            sp.dma_start(wkvg_f[:], wkvg).then_inc(wkvg_in, 16)
            load_x(2)
            sp.dma_start(cst[:], consts).then_inc(consts_in, 16)
            load_x(3)
            sp.dma_start(wq_f[:], wq).then_inc(wq_in, 16)
            sp.dma_start(wo_f[:], wo).then_inc(wo_in, 16)

            def load_weights(e, par):
                sp.dma_start(w1_f[par][:], w1_rows[bass.ds(e * D, D), :]).then_inc(w1_in[par], 16)
                sp.dma_start(w2_f[par][:].rearrange("p (c o) -> p c o", c=KC), w2_view[:, bass.ds(e * KC, KC), :]
                             ).then_inc(w2_in[par], 16)

            def load_bias(e, par):
                sp.dma_start(b1_f[par][:], b1[bass.ds(e * P, P), :]).then_inc(b1_in[par], 16)

            for e in range(2):
                load_weights(e, e)
                load_bias(e, e)
            sp.wait_ge(gatesT_copied, 1)
            sp.dma_start(gates_dram, gatesT[:]).then_inc(gates_out, 16)
            sp.wait_ge(gates_out, 16)

            def load_gate_row(e, par):
                sp.dma_start(gate_row[par][:].rearrange("p (t c) -> p t c", c=P),
                             gates_dram[bass.ds(e * T, T), :].partition_broadcast(P)
                             ).then_inc(gate_row_in[par], 16)

            load_gate_row(0, 0)
            load_gate_row(1, 1)
            with sp.Fori(1, PAIRS) as p:
                for par in range(2):
                    sp.wait_ge(w2_split, 2 * p + par - 1)
                    load_weights(2 * p + par, par)
                    sp.wait_ge(acc_done, (2 * p + par - 1) * NBLK)
                    load_bias(2 * p + par, par)
                    load_gate_row(2 * p + par, par)
            for k in range(NBLK):
                sp.wait_ge(res_done, k + 1)
                sp.dma_start(out_view[:, 2 * k:2 * k + 2],
                             res[:, 4 * k:4 * k + 4, :].rearrange("p (b r) d -> p b r d", r=R)
                             ).then_inc(out_written, 16)
            sp.wait_ge(out_written, 16 * NBLK)

        @block.gpsimd
        def _(pool):
            nc.gpsimd.memset(eps[:], LN_EPS).then_inc(eps_set, 1)
            nc.gpsimd.memset(ones[:], 1.0).then_inc(ones_set, 1)
            nc.gpsimd.memset(vext[:, :, D:NV], 1.0).then_inc(ones_set, 1)

            def normalise(k):
                ts = slice(4 * k, 4 * k + 4)
                pool.wait_ge(rstd_done, k + 1)
                nc.gpsimd.tensor_tensor(xn[:, ts, :], x_tok[:, ts, :], mean_var[:, ts, 0:1].to_broadcast([P, 4, D]),
                                        ALU.subtract).then_inc(centred, 1)
                pool.wait_ge(centred, k)
                nc.gpsimd.tensor_tensor(xn[:, ts, :], xn[:, ts, :], rstd[:, ts].unsqueeze(2).to_broadcast([P, 4, D]),
                                        ALU.mult).then_inc(xn_pool_done, 1)

            def split_weights(e, par, rounds):
                for f, hi, lo, arrived, hi_done, split in (
                        (w1_f[par], w1_hi[par], w1_lo[par], w1_in[par], w1_hi_done, w1_split),
                        (w2_f[par], w2_hi[par], w2_lo[par], w2_in[par], w2_hi_done, w2_split)):
                    pool.wait_ge(arrived, 16 * rounds)
                    nc.gpsimd.tensor_tensor(hi[:], f[:], ones[:, 0:f.shape[1]], ALU.mult).then_inc(hi_done, 1)
                    pool.wait_ge(hi_done, e + 1)
                    nc.gpsimd.tensor_tensor(lo[:], f[:], hi[:].bitcast(F32), ALU.subtract).then_inc(split, 1)

            def gate_first(blk):
                pool.wait_ge(gated_done, blk + 1)
                pool.wait_ge(gate_row_in[0], 16)
                cols = acc[:, blk_cols(blk)]
                nc.gpsimd.tensor_tensor(cols, cols, gate_row[0][:, blk_cols(blk)], ALU.mult).then_inc(acc_done, 1)

            def accumulate(u, j):
                pool.wait_ge(gated_done, u + 1)
                pool.wait_ge(acc_done, u - NBLK + 1)
                cols = acc[:, blk_cols(j % NBLK)]
                nc.gpsimd.tensor_tensor(cols, cols, y[j % 4][:], ALU.add).then_inc(acc_done, 1)

            pool.wait_ge(ones_set, 2)
            def lo_of_weights(f, hi, lo, hi_done, split):
                pool.wait_ge(hi_done, 1)
                nc.gpsimd.tensor_tensor(lo[:], f[:], hi[:].bitcast(F32), ALU.subtract).then_inc(split, 1)

            lo_of_weights(wkvg_f, wkvg_hi, wkvg_lo, wkvg_hi_done, wkvg_split)
            normalise(1)
            lo_of_weights(wq_f, wq_hi, wq_lo, wq_hi_done, wq_split)
            normalise(2)
            normalise(3)
            split_weights(0, 0, 1)
            split_weights(1, 1, 1)
            pool.wait_ge(l1_done, NBLK * KC)
            pool.wait_ge(l2_done, NBLK)
            split_weights(2, 0, 2)
            for u in range(NBLK):
                gate_first(u)
            for u in range(NBLK, 2 * NBLK):
                accumulate(u, u)
            pool.wait_ge(l1_done, 2 * NBLK * KC)
            pool.wait_ge(l2_done, 2 * NBLK)
            split_weights(3, 1, 2)
            for u in range(2 * NBLK, 3 * NBLK):
                accumulate(u, u)
            with pool.Fori(2, PAIRS) as p:
                for par in range(2):
                    pool.wait_ge(l1_done, (2 * p + par - 1) * NBLK * KC)
                    pool.wait_ge(l2_done, (2 * p + par - 1) * NBLK)
                    split_weights(2 * p + par, par, p + 1)
                    for j in range(NBLK):
                        accumulate((2 * p + par - 1) * NBLK + j, j)
            for u in range(UNITS - NBLK, UNITS - 1):
                accumulate(u, u)

        def act_relu_and_hi(act, u, j, rounds):
            i = j % 2
            if j % NBLK == 0:
                act.wait_ge(b1_in[j // NBLK % 2], 16 * rounds)
            for c in range(KC):
                act.wait_ge(l1_done, u * KC + c + 1)
                nc.scalar.activation(h_ps[i][:, c, :], h_ps[i][:, c, :], ACT.Relu,
                                     bias=b1_f[j // NBLK % 2][:, c:c + 1]).then_inc(relu_done, 1)
                act.wait_ge(relu_done, u * KC + c + 1)
                if past(u, 2):
                    act.wait_ge(l2_done, u - 1)
                nc.scalar.copy(h_hi[i][:, c, :], h_ps[i][:, c, :]).then_inc(hhi_done, 1)

        @block.scalar
        def _(act):
            act.wait_ge(eps_set, 1)
            nc.scalar.activation(warm[:, 0:1], eps[:], ACT.Sqrt).then_inc(warm_done, 1)
            act.dma_start(gate_bias[:], gate_b.partition_broadcast(P)).then_inc(gate_b_in, 16)
            act.dma_start(b2_f[:], b2).then_inc(b2_in, 16)

            def deviation(k):
                act.wait_ge(meanvar_done, 4 * k + 4)
                nc.scalar.activation(std[:, 4 * k:4 * k + 4], mean_var[:, 4 * k:4 * k + 4, 1], ACT.Sqrt,
                                     bias=eps[:, 0:1]).then_inc(std_done, 1)

            def hi_of_weights(f, hi, arrived, hi_done):
                act.wait_ge(arrived, 16)
                nc.scalar.copy(hi[:], f[:]).then_inc(hi_done, 1)

            def hi_of_x(k):
                act.wait_ge(xT_done, k + 1)
                nc.scalar.copy(x_hi[:, blk_cols(k)], xT_ps[k % 2]).then_inc(xhi_done, 1)

            def exp_k_and_v(b):
                ts = slice(2 * b, 2 * b + 2)
                act.wait_ge(kvg_done, b + 1)
                nc.scalar.activation(kf[:, ts, :], kvg_ps[b % 2][:, :, 0:D], ACT.Relu, scale=-1.0
                                     ).then_inc(kneg_done, 1)
                nc.scalar.copy(vext[:, ts, 0:D], kvg_ps[b % 2][:, :, D:2 * D]).then_inc(v_done, 1)
                act.wait_ge(kneg_done, b + 1)
                nc.scalar.activation(kf[:, ts, :], kf[:, ts, :], ACT.Exp, scale=-1.0).then_inc(kexp_done, 1)

            def exp_q(k):
                act.wait_ge(q_done, k + 1)
                nc.scalar.activation(qf[:, blk_cols(k)], q_ps, ACT.Relu, scale=-1.0).then_inc(qneg_done, 1)
                act.wait_ge(qneg_done, k + 1)
                nc.scalar.activation(qf[:, blk_cols(k)], qf[:, blk_cols(k)], ACT.Exp, scale=-1.0
                                     ).then_inc(qexp_done, 1)

            def copy_att(k):
                act.wait_ge(attT_done, k + 1)
                nc.scalar.copy(attT[:, blk_cols(k)], att_ps).then_inc(attT_copied, 1)

            deviation(0)
            hi_of_weights(wkvg_f, wkvg_hi, wkvg_in, wkvg_hi_done)
            deviation(1)
            hi_of_weights(wq_f, wq_hi, wq_in, wq_hi_done)
            hi_of_x(0)
            deviation(2)
            deviation(3)
            nc.scalar.activation(warm[:, 1:2], eps[:], ACT.Exp).then_inc(warm_done, 1)
            hi_of_x(1)
            exp_k_and_v(0)
            exp_k_and_v(1)
            exp_q(0)
            hi_of_x(2)
            exp_k_and_v(2)
            exp_k_and_v(3)
            exp_q(1)
            hi_of_x(3)
            exp_k_and_v(4)
            exp_k_and_v(5)
            exp_q(2)
            exp_k_and_v(6)
            exp_k_and_v(7)
            exp_q(3)
            act_relu_and_hi(act, 0, 0, 1)
            act.wait_ge(gate_step, 1)
            nc.scalar.activation(expd[:], shifted[:], ACT.Exp).then_inc(exp_done, 1)
            act_relu_and_hi(act, 1, 1, 1)
            act.wait_ge(gatesT_done, 1)
            nc.scalar.copy(gatesT[:], gatesT_ps).then_inc(gatesT_copied, 1)
            copy_att(0)
            for u in range(2, UPP):
                act_relu_and_hi(act, u, u, 1)
                if u % 2 == 1:
                    copy_att(u // 2)
            with act.Fori(1, PAIRS) as p:
                for j in range(UPP):
                    act_relu_and_hi(act, UPP * p + j, j, p + 1)

        def mask_kv(dve, k):
            dve.wait_ge(kv_done, k + 1)
            if k == 0:
                dve.wait_ge(consts_in, 16)
            nc.vector.tensor_tensor(kv[:, 2 * k:2 * k + 2, :],
                                    att_ps.rearrange("p (b n) -> p b n", b=2)[:, :, 0:NV],
                                    kv_mask.unsqueeze(1).to_broadcast([P, 2, NV]), ALU.mult
                                    ).then_inc(kvmask_done, 1)

        @block.vector
        def _(dve):
            def statistics(k):
                dve.wait_ge(x_in[k], 16)
                for t in range(4 * k, 4 * k + 4):
                    nc.vector.bn_stats(stats[:, t, :], x_tok[:, t, :]).then_inc(stats_done, 1)
                for t in range(4 * k, 4 * k + 4):
                    dve.wait_ge(stats_done, t + 1)
                    nc.vector.bn_aggr(mean_var[:, t, :], stats[:, t, :]).then_inc(meanvar_done, 1)

            def lo_of_x(k):
                dve.wait_ge(xhi_done, k + 1)
                nc.vector.tensor_tensor(x_lo[:, blk_cols(k)], xT_ps[k % 2], x_hi[:, blk_cols(k)].bitcast(F32),
                                        ALU.subtract).then_inc(xlo_done, 1)

            def finish_k(b):
                ts = slice(2 * b, 2 * b + 2)
                dve.wait_ge(kexp_done, b + 1)
                dve.wait_ge(v_done, b + 1)
                if b == 0:
                    dve.wait_ge(gate_b_in, 16)
                nc.vector.tensor_tensor(logits[:, ts, :], kvg_ps[b % 2][:, :, 2 * D:KVG],
                                        gate_bias[:].unsqueeze(1).to_broadcast([P, 2, E]), ALU.add
                                        ).then_inc(logits_done, 1)
                nc.vector.scalar_tensor_tensor(out=kf[:, ts, :], in0=kvg_ps[b % 2][:, :, 0:D], scalar=0.0,
                                               in1=kf[:, ts, :], op0=ALU.max, op1=ALU.add
                                               ).then_inc(kf_done, 1)
                dve.wait_ge(logits_done, b + 1)
                for t in (2 * b, 2 * b + 1):
                    nc.vector.max(top8[:, t, :], logits[:, t, :]).then_inc(top_done, 1)
                for t in (2 * b, 2 * b + 1):
                    dve.wait_ge(top_done, t + 1)
                    nc.vector.max_index(idx8[:, t, :], top8[:, t, :], logits[:, t, :]).then_inc(idx_done, 1)

            def finish_q(k):
                dve.wait_ge(qexp_done, k + 1)
                nc.vector.scalar_tensor_tensor(out=qf[:, blk_cols(k)], in0=q_ps, scalar=0.0,
                                               in1=qf[:, blk_cols(k)], op0=ALU.max, op1=ALU.add
                                               ).then_inc(qf_done, 1)

            def inverse_deviation(k):
                dve.wait_ge(std_done, k + 1)
                nc.vector.reciprocal(rstd[:, 4 * k:4 * k + 4], std[:, 4 * k:4 * k + 4]).then_inc(rstd_done, 1)

            def normalise_first():
                dve.wait_ge(rstd_done, 1)
                for t in range(4):
                    nc.vector.tensor_scalar(xn[:, t, :], x_tok[:, t, :], mean_var[:, t, 0:1], rstd[:, t:t + 1],
                                            ALU.subtract, ALU.mult).then_inc(xn_done, 1)

            def shift_logits():
                dve.wait_ge(top_done, T)
                nc.vector.tensor_tensor(shifted[:], logits[:], top8[:, :, 0:1].to_broadcast([P, T, E]),
                                        ALU.subtract).then_inc(gate_step, 1)

            def gate_values():
                dve.wait_ge(idx_done, T)
                nc.vector.tensor_copy(idxf[:, :, 0:TOP], idx8[:, :, 0:TOP]).then_inc(gate_step, 1)
                all_ramp = ramp.unsqueeze(1).to_broadcast([P, T, E])
                dve.wait_ge(gate_step, 2)
                nc.vector.tensor_tensor(is_first[:], all_ramp, idxf[:, :, 0:1].to_broadcast([P, T, E]),
                                        ALU.is_equal).then_inc(gate_step, 1)
                nc.vector.tensor_tensor(is_second[:], all_ramp, idxf[:, :, 1:2].to_broadcast([P, T, E]),
                                        ALU.is_equal).then_inc(gate_step, 1)
                dve.wait_ge(exp_done, 1)
                nc.vector.reduce_sum(expsum[:], expd[:], AX_X).then_inc(gate_step, 1)
                dve.wait_ge(gate_step, 4)
                nc.vector.tensor_tensor(picked[:], is_first[:], is_second[:], ALU.add).then_inc(gate_step, 1)
                dve.wait_ge(gate_step, 5)
                nc.vector.reciprocal(rexpsum[:], expsum[:]).then_inc(gate_step, 1)
                dve.wait_ge(gate_step, 6)
                nc.vector.tensor_tensor(picked[:], expd[:], picked[:], ALU.mult).then_inc(gate_step, 1)
                dve.wait_ge(gate_step, 8)
                nc.vector.tensor_tensor(gates[:].rearrange("p e t -> p t e"), picked[:],
                                        rexpsum[:].unsqueeze(2).to_broadcast([P, T, E]), ALU.mult
                                        ).then_inc(gates_done, 1)

            def divide(b):
                ts = slice(2 * b, 2 * b + 2)
                both = num_ps[:, 0:2 * NV].rearrange("p (r n) -> p r n", r=2)
                dve.wait_ge(num_done, b + 1)
                nc.vector.tensor_scalar(den[:, ts, :], both[:, :, D:NV], DEN_EPS, None, ALU.add
                                        ).then_inc(den_done, 1)
                dve.wait_ge(den_done, b + 1)
                nc.vector.reciprocal(rden[:, ts, :], den[:, ts, :]).then_inc(rden_done, 1)
                dve.wait_ge(rden_done, b + 1)
                for r in range(2):
                    t = 2 * b + r
                    last = nc.vector.tensor_tensor(
                        att[:, t, :].rearrange("p (h d) -> p h d", h=HEADS),
                        both[:, r, 0:D].rearrange("p (h d) -> p h d", h=HEADS),
                        rden[:, t, :].unsqueeze(2).to_broadcast([P, HEADS, D // HEADS]), ALU.mult)
                    last.then_inc(att_done, 1)

            def add_residual(k):
                dve.wait_ge(wo_done, k + 1)
                cols = x_tok[:, 4 * k:4 * k + 4, :]
                nc.vector.tensor_tensor(cols, cols, att_ps.rearrange("p (t d) -> p t d", t=4), ALU.add
                                        ).then_inc(residual_done, 1)

            def lo_of_h(u, j):
                i = j % 2
                for c in range(KC):
                    dve.wait_ge(hhi_done, u * KC + c + 1)
                    nc.vector.tensor_tensor(h_lo[i][:, c, :], h_ps[i][:, c, :], h_hi[i][:, c, :].bitcast(F32),
                                            ALU.subtract).then_inc(hlo_done, 1)

            def gate_output(u, j, e, rounds):
                blk = j % NBLK
                par = j // NBLK % 2
                dve.wait_ge(l2_done, u + 1)
                if blk == 0:
                    dve.wait_ge(gate_row_in[par], rounds * 16)
                if past(u, 2 * NBLK):
                    dve.wait_ge(acc_done, u - NBLK + 1)
                nc.vector.scalar_tensor_tensor(out=y[j % 4][:], in0=y_ps[j % 2], scalar=b2_f[:, bass.ds(e, 1)],
                                               in1=gate_row[par][:, blk_cols(blk)], op0=ALU.add, op1=ALU.mult
                                               ).then_inc(gated_done, 1)

            def first_output(u):
                dve.wait_ge(l2_done, u + 1)
                if u == 0:
                    dve.wait_ge(b2_in, 16)
                nc.vector.tensor_scalar(acc[:, blk_cols(u)], y_ps[u % 2], b2_f[:, 0:1], None, ALU.add
                                        ).then_inc(gated_done, 1)

            statistics(0)
            inverse_deviation(0)
            normalise_first()
            statistics(1)
            inverse_deviation(1)
            statistics(2)
            inverse_deviation(2)
            lo_of_x(0)
            statistics(3)
            inverse_deviation(3)
            lo_of_x(1)
            finish_k(0)
            finish_k(1)
            finish_q(0)
            lo_of_x(2)
            finish_k(2)
            finish_k(3)
            mask_kv(dve, 0)
            finish_q(1)
            lo_of_x(3)
            finish_k(4)
            finish_k(5)
            mask_kv(dve, 1)
            finish_q(2)
            finish_k(6)
            finish_k(7)
            finish_q(3)
            shift_logits()
            mask_kv(dve, 2)
            divide(0)
            lo_of_h(0, 0)
            mask_kv(dve, 3)
            divide(1)
            gate_values()
            lo_of_h(1, 1)
            divide(2)
            first_output(0)
            for u in range(2, UPP):
                if u + 1 < B:
                    divide(u + 1)
                lo_of_h(u, u)
                if u - 1 < NBLK:
                    first_output(u - 1)
                else:
                    gate_output(u - 1, u - 1, (u - 1) // NBLK, 1)
                if u % 2 == 0:
                    add_residual(u // 2 - 1)
            add_residual(NBLK - 1)
            with dve.Fori(1, PAIRS) as p:
                for j in range(UPP):
                    lo_of_h(UPP * p + j, j)
                    if j == 0:
                        gate_output(UPP * p - 1, UPP - 1, 2 * p - 1, p)
                    else:
                        gate_output(UPP * p + (j - 1), j - 1, 2 * p + (j - 1) // NBLK, p + 1)
            def finish(k):
                dve.wait_ge(fin_done, k + 1)
                nc.vector.tensor_tensor(res[:, 4 * k:4 * k + 4, :],
                                        fin_ps[k % 2].rearrange("p (t d) -> p t d", t=4),
                                        x_tok[:, 4 * k:4 * k + 4, :], ALU.add).then_inc(res_done, 1)

            finish(0)
            gate_output(UNITS - 1, UPP - 1, E - 1, PAIRS)
            dve.wait_ge(gated_done, UNITS)
            dve.wait_ge(acc_done, UNITS - NBLK)
            last_cols = acc[:, blk_cols(NBLK - 1)]
            nc.vector.tensor_tensor(last_cols, last_cols, y[(UNITS - 1) % 4][:], ALU.add).then_inc(last_acc_done, 1)
            finish(1)
            finish(2)
            finish(3)

        @block.tensor
        def _(pe):
            def three(out_ap, lhs_hi, lhs_lo, rhs_hi, rhs_lo, start=True, stop=True):
                nc.tensor.matmul(out_ap, lhs_hi, rhs_hi, start=start, stop=False)
                nc.tensor.matmul(out_ap, lhs_hi, rhs_lo, start=False, stop=False)
                return nc.tensor.matmul(out_ap, lhs_lo, rhs_hi, start=False, stop=stop)

            def transpose_x(k):
                if k == 0:
                    pe.wait_ge(consts_in, 16)
                pe.wait_ge(xn_done, 4) if k == 0 else pe.wait_ge(xn_pool_done, k)
                if k >= 2:
                    pe.wait_ge(xlo_done, k - 1)
                for t in range(4):
                    last = nc.tensor.transpose(xT_ps[k % 2][:, t * P:(t + 1) * P], xn[:, 4 * k + t, :], ident)
                last.then_inc(xT_done, 1)

            def project_kvg(b):
                if b == 0:
                    pe.wait_ge(wkvg_split, 1)
                pe.wait_ge(xlo_done, b // 2 + 1)
                if b >= 2:
                    pe.wait_ge(kf_done, b - 1)
                for r in range(2):
                    cols = slice((2 * b + r) * P, (2 * b + r + 1) * P)
                    last = three(kvg_ps[b % 2][:, r, 0:KVG], x_hi[:, cols], x_lo[:, cols], wkvg_hi[:], wkvg_lo[:])
                last.then_inc(kvg_done, 1)

            def project_q(k):
                if k == 0:
                    pe.wait_ge(wq_split, 1)
                else:
                    pe.wait_ge(qf_done, k)
                pe.wait_ge(xlo_done, k + 1)
                three(q_ps, wq_hi[:], wq_lo[:], x_hi[:, blk_cols(k)], x_lo[:, blk_cols(k)]).then_inc(q_done, 1)

            def keys_values(k):
                pe.wait_ge(kf_done, 2 * k + 2)
                if k == 0:
                    pe.wait_ge(ones_set, 2)
                else:
                    pe.wait_ge(kvmask_done, k)
                for b in range(2):
                    for r in range(2):
                        t = 4 * k + 2 * b + r
                        last = nc.tensor.matmul(att_ps[:, 256 * b:256 * b + NV], kf[:, t, :], vext[:, t, :],
                                                start=(r == 0), stop=(r == 1))
                last.then_inc(kv_done, 1)

            def numerator(b):
                pe.wait_ge(kvmask_done, b // 2 + 1)
                if b == 0:
                    pe.wait_ge(qf_done, NBLK)
                else:
                    pe.wait_ge(att_done, 2 * b)
                for r in range(2):
                    t = 2 * b + r
                    last = nc.tensor.matmul(num_ps[:, r * NV:(r + 1) * NV], qf[:, t * P:(t + 1) * P], kv[:, b, :],
                                            start=True, stop=True)
                last.then_inc(num_done, 1)

            def transpose_att(k):
                pe.wait_ge(att_done, 4 * k + 4)
                if k >= 1:
                    pe.wait_ge(residual_done, k)
                for t in range(4):
                    last = nc.tensor.transpose(att_ps[:, t * P:(t + 1) * P], att[:, 4 * k + t, :], ident)
                last.then_inc(attT_done, 1)

            def project_out(k):
                if k == 0:
                    pe.wait_ge(wo_in, 16)
                pe.wait_ge(attT_copied, k + 1)
                for t in range(4):
                    last = nc.tensor.matmul(att_ps[:, t * P:(t + 1) * P], attT[:, (4 * k + t) * P:(4 * k + t + 1) * P],
                                            wo_f[:], start=True, stop=True)
                last.then_inc(wo_done, 1)

            def first_product(u, j, e):
                par, blk, i = j // NBLK % 2, j % NBLK, j % 2
                if blk == 0:
                    pe.wait_ge(w1_split, e + 1)
                if past(u, 2):
                    pe.wait_ge(hlo_done, (u - 1) * KC)
                elif u == 0:
                    pe.wait_ge(xlo_done, NBLK)
                else:
                    pe.wait_ge(kf_done, B - 1)
                for c in range(KC):
                    w = slice(c * P, (c + 1) * P)
                    three(h_ps[i][:, c, :], w1_hi[par][:, w], w1_lo[par][:, w],
                          x_hi[:, blk_cols(blk)], x_lo[:, blk_cols(blk)]).then_inc(l1_done, 1)

            def second_product(u, j, e):
                par, blk, i = j // NBLK % 2, j % NBLK, j % 2
                if blk == 0:
                    pe.wait_ge(w2_split, e + 1)
                if past(u, 2):
                    pe.wait_ge(gated_done, u - 1)
                elif u == 0:
                    pe.wait_ge(kf_done, B)
                else:
                    pe.wait_ge(gatesT_copied, 1)
                for c in range(KC):
                    w = slice(c * D, (c + 1) * D)
                    pe.wait_ge(hlo_done, u * KC + c + 1)
                    last = three(y_ps[i], w2_hi[par][:, w], w2_lo[par][:, w], h_hi[i][:, c, :], h_lo[i][:, c, :],
                                 start=(c == 0), stop=(c == KC - 1))
                last.then_inc(l2_done, 1)

            def warm_up():
                pe.wait_ge(ones_set, 1)
                for _ in range(WARM_UPS):
                    last = nc.tensor.matmul(att_ps[:, 0:P], ones[:, 0:P], ones[:, 0:P], start=True, stop=True)
                last.then_inc(pe_warm, 1)

            def transpose_gates():
                pe.wait_ge(gates_done, 1)
                pe.wait_ge(kf_done, B)
                nc.tensor.transpose(gatesT_ps, gates[:].rearrange("p e t -> p (e t)"), ident).then_inc(gatesT_done, 1)

            warm_up()
            transpose_x(0)
            transpose_x(1)
            project_kvg(0)
            project_kvg(1)
            project_q(0)
            transpose_x(2)
            project_kvg(2)
            project_kvg(3)
            keys_values(0)
            project_q(1)
            transpose_x(3)
            project_kvg(4)
            project_kvg(5)
            keys_values(1)
            project_q(2)
            project_kvg(6)
            project_kvg(7)
            project_q(3)
            first_product(0, 0, 0)
            keys_values(2)
            numerator(0)
            first_product(1, 1, 0)
            keys_values(3)
            numerator(1)
            second_product(0, 0, 0)
            transpose_gates()
            numerator(2)
            transpose_att(0)
            for u in range(2, UPP):
                first_product(u, u, u // NBLK)
                if u == 2:
                    numerator(3)
                if u % 2 == 1:
                    transpose_att(u // 2)
                else:
                    project_out(u // 2 - 1)
                second_product(u - 1, u - 1, (u - 1) // NBLK)
                if u + 2 < B:
                    numerator(u + 2)
            project_out(NBLK - 1)
            with pe.Fori(1, PAIRS) as p:
                for j in range(UPP):
                    first_product(UPP * p + j, j, 2 * p + j // NBLK)
                    if j == 0:
                        second_product(UPP * p - 1, UPP - 1, 2 * p - 1)
                    else:
                        second_product(UPP * p + (j - 1), j - 1, 2 * p + (j - 1) // NBLK)
            def turn_back(k):
                if k < NBLK - 1:
                    pe.wait_ge(acc_done, UNITS - NBLK + k + 1)
                else:
                    pe.wait_ge(last_acc_done, 1)
                if k >= 2:
                    pe.wait_ge(res_done, k - 1)
                for t in range(4):
                    last = nc.tensor.transpose(fin_ps[k % 2][:, t * P:(t + 1) * P],
                                               acc[:, (4 * k + t) * P:(4 * k + t + 1) * P], ident)
                last.then_inc(fin_done, 1)

            turn_back(0)
            turn_back(1)
            second_product(UNITS - 1, UPP - 1, E - 1)
            turn_back(2)
            turn_back(3)


def kernel(L0_attn_x, L0_attn_Wq, L0_attn_Wk, L0_attn_Wv, L0_attn_Wo, L0_ffn_gate_w, L0_ffn_gate_b,
           L0_ffn_w1, L0_ffn_b1, L0_ffn_w2, L0_ffn_b2):
    import concourse.bacc as bacc
    from concourse.bass_utils import run_bass_kernel_spmd

    x = np.ascontiguousarray(L0_attn_x)
    E, D, H = L0_ffn_w1.shape
    T = x.shape[0] * x.shape[1] // P
    arrays = {
        "x": x,
        "wkvg": np.ascontiguousarray(np.concatenate(
            [np.asarray(L0_attn_Wk), np.asarray(L0_attn_Wv), np.asarray(L0_ffn_gate_w).T], axis=1)),
        "wq": np.ascontiguousarray(L0_attn_Wq),
        "wo": np.ascontiguousarray(L0_attn_Wo),
        "gate_b": np.ascontiguousarray(L0_ffn_gate_b),
        "w1": np.ascontiguousarray(L0_ffn_w1),
        "b1": np.ascontiguousarray(np.asarray(L0_ffn_b1).reshape(E, H // P, P).transpose(0, 2, 1)).reshape(E * P, H // P),
        "w2": np.ascontiguousarray(L0_ffn_w2),
        "b2": np.ascontiguousarray(np.asarray(L0_ffn_b2).T),
        "consts": shape_constants(D),
    }
    nc = bacc.Bacc("TRN2", target_bir_lowering=False, num_devices=1)
    args = [nc.dram_tensor(f"in_{n}", a.shape, mybir.dt.from_np(a.dtype), kind="ExternalInput").ap()
            for n, a in arrays.items()]
    gates_dram = nc.dram_tensor("gates_dram", (E * T, P), F32, kind="Internal").ap()
    out = nc.dram_tensor("out", x.shape, F32, kind="ExternalOutput").ap()
    linear_attention_with_top2_experts(nc, *args, gates_dram, out)
    r = run_bass_kernel_spmd(nc, [{f"in_{n}": a for n, a in arrays.items()}], core_ids=[0])
    return np.asarray(r.results[0]["out"])
```

```python
from contextlib import ExitStack

import numpy as np

import concourse.bass as bass
from concourse import mybir

F32 = mybir.dt.float32
F32R = mybir.dt.float32r
U32 = mybir.dt.uint32
ALU = mybir.AluOpType
ACT = mybir.ActivationFunctionType
AX_X = mybir.AxisListType.X

P = 128
HEADS = 16
TOP = 2
LN_EPS = 1e-5
DEN_EPS = 1e-6


def shape_constants(D):
    rows = np.arange(D)
    head = rows // (D // HEADS)
    ident = np.eye(D, dtype=np.float32)
    same_head = (head[:, None] == head[None, :]).astype(np.float32)
    of_head = (head[:, None] == np.arange(HEADS)[None, :]).astype(np.float32)
    ramp = np.broadcast_to(np.arange(8, dtype=np.float32), (D, 8))
    return np.ascontiguousarray(np.concatenate([ident, same_head, of_head, ramp], axis=1))


def linear_attention_with_top2_experts(nc, x, wkvg, wq, wo, gate_b, w1, b1, w2, b2, consts, gates_dram, out):
    B, S, D = x.shape
    E, _, H = w1.shape
    T = B * S // P
    NBLK = T // 4
    BW = 4 * P
    R = S // P
    KC = H // P
    KVG = 2 * D + E
    PARTS = [(0, 2), (2, 4), (4, 8), (8, 12), (12, 16)]
    NV = D + HEADS
    UNITS = E * NBLK
    PAIRS = E // 2
    UPP = 2 * NBLK
    WARM_UPS_BEFORE, WARM_UPS_AFTER = 9, 6
    assert D == P and R == 2 and KC == 2 and NBLK == 4 and E == 8
    assert PARTS[-1][1] == T

    x_view = x.rearrange("b (p r) d -> p b r d", r=R)
    out_view = out.rearrange("b (p r) d -> p b r d", r=R)
    w1_rows = w1.rearrange("e d h -> (e d) h")
    w2_view = w2.rearrange("e (c p) o -> p (e c) o", p=P)

    with ExitStack() as ctx:
        def sb(name, shape, dt=F32):
            return ctx.enter_context(nc.sbuf_tensor(name, shape, dt))

        def sem(name):
            return ctx.enter_context(nc.semaphore(name))

        x_tok = sb("x_tok", [P, T, D])
        xn = sb("xn", [P, T, D])
        x_hi = sb("x_hi", [P, T * P], F32R)
        x_lo = sb("x_lo", [P, T * P], F32R)
        cst = sb("cst", [P, D + NV + 8])
        wkvg_f = sb("wkvg_f", [P, KVG])
        wkvg_hi = sb("wkvg_hi", [P, KVG], F32R)
        wkvg_lo = sb("wkvg_lo", [P, KVG], F32R)
        wq_f = sb("wq_f", [P, D])
        wq_hi = sb("wq_hi", [P, D], F32R)
        wq_lo = sb("wq_lo", [P, D], F32R)
        wo_f = sb("wo_f", [P, D])
        wo_hi = sb("wo_hi", [P, D], F32R)
        wo_lo = sb("wo_lo", [P, D], F32R)
        gate_bias = sb("gate_bias", [P, E])
        b2_f = sb("b2_f", [P, E])
        w1_f = [sb(f"w1_f{i}", [P, H]) for i in range(2)]
        w2_f = [sb(f"w2_f{i}", [P, KC * D]) for i in range(2)]
        b1_f = [sb(f"b1_f{i}", [P, KC]) for i in range(2)]
        w1_hi = [sb(f"w1_hi{i}", [P, H], F32R) for i in range(2)]
        w1_lo = [sb(f"w1_lo{i}", [P, H], F32R) for i in range(2)]
        w2_hi = [sb(f"w2_hi{i}", [P, KC * D], F32R) for i in range(2)]
        w2_lo = [sb(f"w2_lo{i}", [P, KC * D], F32R) for i in range(2)]
        stats = sb("stats", [P, T, 6])
        mean_var = sb("mean_var", [P, T, 2])
        eps = sb("eps", [P, 1])
        ones = sb("ones", [P, KVG])
        warm = sb("warm", [P, 2])
        std = sb("std", [P, T])
        rstd = sb("rstd", [P, T])
        offset = sb("offset", [P, 8])
        minus_half = sb("minus_half", [P, 4])
        qf = sb("qf", [P, T * P])
        kf = sb("kf", [P, T, D])
        vext = sb("vext", [P, T, NV])
        kv = sb("kv", [P, B, NV])
        den = sb("den", [P, T, HEADS])
        rden = sb("rden", [P, T, HEADS])
        att = sb("att", [P, T, D])
        attT_hi = sb("attT_hi", [P, T * P], F32R)
        attT_lo = sb("attT_lo", [P, T * P], F32R)
        attn = sb("attn", [P, T * P])
        logits = sb("logits", [P, T, E])
        top8 = sb("top8", [P, T, 8])
        idx8 = sb("idx8", [P, T, 8], U32)
        idxf = sb("idxf", [P, T, 8])
        shifted = sb("shifted", [P, T, E])
        expd = sb("expd", [P, T, E])
        expsum = sb("expsum", [P, T])
        rexpsum = sb("rexpsum", [P, T])
        is_first = sb("is_first", [P, T, E])
        is_second = sb("is_second", [P, T, E])
        picked = sb("picked", [P, T, E])
        gates = sb("gates", [P, E, T])
        gatesT = sb("gatesT", [P, P])
        gate_row = [sb(f"gate_row{i}", [P, T * P]) for i in range(2)]
        h_hi = [sb(f"h_hi{i}", [P, KC, BW], F32R) for i in range(2)]
        h_lo = [sb(f"h_lo{i}", [P, KC, BW], F32R) for i in range(2)]
        y = [sb(f"y{i}", [P, BW]) for i in range(4)]
        acc = sb("acc", [P, T * P])
        res = sb("res", [P, T, D])

        ident = cst[:, 0:D]
        kv_mask = cst[:, D:D + NV]
        ramp = cst[:, D + NV:D + NV + 8]

        banks = ctx.enter_context(nc.psum_tensor("banks", [P, 8, 512], F32))
        xT_ps = [banks[:, i, :] for i in (0, 7, 1, 0, 1)]
        q_ps = banks[:, 7, :]
        kvg_ps = [banks[:, 2:4, :], banks[:, 4:6, :]]
        att_ps = banks[:, 6, :]
        num_ps = banks[:, 7, :]
        h_ps = [banks[:, 0:2, :], banks[:, 2:4, :]]
        y_ps = [banks[:, 4, :], banks[:, 5, :]]
        gatesT_ps = banks[:, 5, 0:P]
        fin_ps = [banks[:, i, :] for i in (6, 7, 0, 1)]

        x_in = [sem(f"x_in{i}") for i in range(len(PARTS))]
        consts_in = sem("consts_in")
        gate_b_in = sem("gate_b_in")
        b1_in = [sem(f"b1_in{i}") for i in range(2)]
        b2_in = sem("b2_in")
        wkvg_in = sem("wkvg_in")
        wq_in = sem("wq_in")
        wo_in = sem("wo_in")
        w1_in = [sem(f"w1_in{i}") for i in range(2)]
        w2_in = [sem(f"w2_in{i}") for i in range(2)]
        eps_set = sem("eps_set")
        ones_set = sem("ones_set")
        stats_done = sem("stats_done")
        meanvar_done = sem("meanvar_done")
        std_done = sem("std_done")
        pe_warm = sem("pe_warm")
        warm_done = sem("warm_done")
        rstd_done = sem("rstd_done")
        rstd_pool_done = sem("rstd_pool_done")
        xn_done = sem("xn_done")
        centred = sem("centred")
        xn_pool_done = sem("xn_pool_done")
        xn_act_done = sem("xn_act_done")
        offset_done = sem("offset_done")
        var_done = sem("var_done")
        xT_done = sem("xT_done")
        xhi_done = sem("xhi_done")
        xlo_done = sem("xlo_done")
        wkvg_hi_done = sem("wkvg_hi_done")
        wkvg_split = sem("wkvg_split")
        wq_hi_done = sem("wq_hi_done")
        wq_split = sem("wq_split")
        w1_hi_done = sem("w1_hi_done")
        w1_split = sem("w1_split")
        w2_hi_done = sem("w2_hi_done")
        w2_split = sem("w2_split")
        q_done = sem("q_done")
        qneg_done = sem("qneg_done")
        qexp_done = sem("qexp_done")
        qf_done = sem("qf_done")
        kvg_done = sem("kvg_done")
        kneg_done = sem("kneg_done")
        kexp_done = sem("kexp_done")
        v_done = sem("v_done")
        kf_done = sem("kf_done")
        logits_done = sem("logits_done")
        kv_done = sem("kv_done")
        kvmask_done = sem("kvmask_done")
        num_done = sem("num_done")
        den_done = sem("den_done")
        rden_done = sem("rden_done")
        att_done = sem("att_done")
        attT_done = sem("attT_done")
        attT_hi_done = sem("attT_hi_done")
        attT_lo_done = sem("attT_lo_done")
        wo_hi_done = sem("wo_hi_done")
        wo_split = sem("wo_split")
        wo_done = sem("wo_done")
        attn_copied = sem("attn_copied")
        attn_added = sem("attn_added")
        top_done = sem("top_done")
        idx_done = sem("idx_done")
        gate_step = sem("gate_step")
        pick_step = sem("pick_step")
        exp_done = sem("exp_done")
        gates_done = sem("gates_done")
        gatesT_done = sem("gatesT_done")
        gatesT_copied = sem("gatesT_copied")
        gates_out = sem("gates_out")
        gate_row_in = [sem(f"gate_row_in{i}") for i in range(2)]
        l1_done = sem("l1_done")
        relu_done = sem("relu_done")
        hhi_done = sem("hhi_done")
        hlo_done = sem("hlo_done")
        l2_done = sem("l2_done")
        gated_done = sem("gated_done")
        acc_done = sem("acc_done")
        last_but_one_acc_done = sem("last_but_one_acc_done")
        fin_done = sem("fin_done")
        fin_copied = sem("fin_copied")
        res_pool_done = sem("res_pool_done")
        res_done = sem("res_done")
        out_written = sem("out_written")

        block = ctx.enter_context(nc.Block())

        def blk_cols(k):
            return slice(k * BW, (k + 1) * BW)

        def part_cols(i):
            return slice(PARTS[i][0] * P, PARTS[i][1] * P)

        def past(u, first):
            return not isinstance(u, int) or u >= first

        @block.sync
        def _(sp):
            def load_x(i):
                a, b = PARTS[i]
                sp.dma_start(x_tok[:, a:b, :].rearrange("p (b r) d -> p b r d", r=R),
                             x_view[:, a // R:b // R]).then_inc(x_in[i], 16)

            load_x(0)
            load_x(1)
            sp.dma_start(cst[:], consts).then_inc(consts_in, 16)
            load_x(2)
            sp.dma_start(wkvg_f[:], wkvg).then_inc(wkvg_in, 16)
            load_x(3)
            load_x(4)
            sp.dma_start(wq_f[:], wq).then_inc(wq_in, 16)
            sp.dma_start(gate_bias[:], gate_b.partition_broadcast(P)).then_inc(gate_b_in, 16)
            sp.dma_start(b2_f[:], b2).then_inc(b2_in, 16)
            sp.dma_start(wo_f[:], wo).then_inc(wo_in, 16)

            def load_weights(e, par):
                sp.dma_start(w1_f[par][:], w1_rows[bass.ds(e * D, D), :]).then_inc(w1_in[par], 16)
                sp.dma_start(w2_f[par][:].rearrange("p (c o) -> p c o", c=KC), w2_view[:, bass.ds(e * KC, KC), :]
                             ).then_inc(w2_in[par], 16)

            def load_bias(e, par):
                sp.dma_start(b1_f[par][:], b1[bass.ds(e * P, P), :]).then_inc(b1_in[par], 16)

            for e in range(2):
                load_weights(e, e)
                load_bias(e, e)
            sp.wait_ge(gatesT_copied, 1)
            sp.dma_start(gates_dram, gatesT[:]).then_inc(gates_out, 16)
            sp.wait_ge(gates_out, 16)

            def load_gate_row(e, par):
                sp.dma_start(gate_row[par][:].rearrange("p (t c) -> p t c", c=P),
                             gates_dram[bass.ds(e * T, T), :].partition_broadcast(P)
                             ).then_inc(gate_row_in[par], 16)

            load_gate_row(0, 0)
            load_gate_row(1, 1)
            with sp.Fori(1, PAIRS) as p:
                for par in range(2):
                    sp.wait_ge(w2_split, 2 * p + par - 1)
                    load_weights(2 * p + par, par)
                    sp.wait_ge(acc_done, (2 * p + par - 1) * NBLK)
                    load_bias(2 * p + par, par)
                    load_gate_row(2 * p + par, par)
            for k in (2, 3):
                sp.wait_ge(res_done, k - 1)
                sp.dma_start(out_view[:, 2 * k:2 * k + 2],
                             res[:, 4 * k:4 * k + 4, :].rearrange("p (b r) d -> p b r d", r=R)
                             ).then_inc(out_written, 16)
            sp.wait_ge(out_written, 16 * NBLK)

        @block.gpsimd
        def _(pool):
            nc.gpsimd.memset(eps[:], LN_EPS).then_inc(eps_set, 1)
            nc.gpsimd.memset(ones[:], 1.0).then_inc(ones_set, 1)
            nc.gpsimd.memset(minus_half[:], -0.5).then_inc(ones_set, 1)
            nc.gpsimd.memset(vext[:, :, D:NV], 1.0).then_inc(ones_set, 1)

            def inverse_deviation(i):
                ts = slice(*PARTS[i])
                pool.wait_ge(meanvar_done, PARTS[i][1])
                nc.gpsimd.tensor_tensor(mean_var[:, ts, 1], mean_var[:, ts, 1], eps[:].to_broadcast([P, 4]), ALU.add
                                        ).then_inc(var_done, 1)
                pool.wait_ge(var_done, i - 2)
                nc.gpsimd.tensor_tensor(rstd[:, ts], mean_var[:, ts, 1], minus_half[:], ALU.pow
                                        ).then_inc(rstd_pool_done, 1)

            def normalise(i):
                ts = slice(*PARTS[i])
                nc.gpsimd.tensor_tensor(xn[:, ts, :], x_tok[:, ts, :], mean_var[:, ts, 0:1].to_broadcast([P, 4, D]),
                                        ALU.subtract).then_inc(centred, 1)
                pool.wait_ge(rstd_pool_done, i - 2)
                pool.wait_ge(centred, i - 2)
                nc.gpsimd.tensor_tensor(xn[:, ts, :], xn[:, ts, :], rstd[:, ts].unsqueeze(2).to_broadcast([P, 4, D]),
                                        ALU.mult).then_inc(xn_pool_done, 1)

            def split_wo():
                pool.wait_ge(wo_in, 16)
                nc.gpsimd.tensor_tensor(wo_hi[:], wo_f[:], ones[:, 0:D], ALU.mult).then_inc(wo_hi_done, 1)
                pool.wait_ge(wo_hi_done, 1)
                nc.gpsimd.tensor_tensor(wo_lo[:], wo_f[:], wo_hi[:].bitcast(F32), ALU.subtract).then_inc(wo_split, 1)

            def split_w1(e, par, rounds):
                pool.wait_ge(w1_in[par], 16 * rounds)
                nc.gpsimd.tensor_tensor(w1_hi[par][:], w1_f[par][:], ones[:, 0:H], ALU.mult).then_inc(w1_hi_done, 1)
                pool.wait_ge(w1_hi_done, e + 1)
                nc.gpsimd.tensor_tensor(w1_lo[par][:], w1_f[par][:], w1_hi[par][:].bitcast(F32), ALU.subtract
                                        ).then_inc(w1_split, 1)

            def split_w2(e, par, rounds):
                pool.wait_ge(w2_in[par], 16 * rounds)
                nc.gpsimd.tensor_tensor(w2_hi[par][:], w2_f[par][:], ones[:, 0:KC * D], ALU.mult
                                        ).then_inc(w2_hi_done, 1)
                pool.wait_ge(w2_hi_done, e + 1)
                nc.gpsimd.tensor_tensor(w2_lo[par][:], w2_f[par][:], w2_hi[par][:].bitcast(F32), ALU.subtract
                                        ).then_inc(w2_split, 1)

            def gate_first(blk):
                pool.wait_ge(gated_done, blk + 1)
                pool.wait_ge(gate_row_in[0], 16)
                cols = acc[:, blk_cols(blk)]
                nc.gpsimd.tensor_tensor(cols, cols, gate_row[0][:, blk_cols(blk)], ALU.mult).then_inc(acc_done, 1)

            def accumulate(u, j):
                pool.wait_ge(gated_done, u + 1)
                pool.wait_ge(acc_done, u - NBLK + 1)
                cols = acc[:, blk_cols(j % NBLK)]
                nc.gpsimd.tensor_tensor(cols, cols, y[j % 4][:], ALU.add).then_inc(acc_done, 1)

            def add_attention(blk):
                pool.wait_ge(attn_copied, blk + 1)
                pool.wait_ge(acc_done, NBLK + blk + 1)
                cols = acc[:, blk_cols(blk)]
                nc.gpsimd.tensor_tensor(cols, cols, attn[:, blk_cols(blk)], ALU.add).then_inc(attn_added, 1)

            pool.wait_ge(ones_set, 3)

            def lo_of_weights(f, hi, lo, hi_done, split):
                pool.wait_ge(hi_done, 1)
                nc.gpsimd.tensor_tensor(lo[:], f[:], hi[:].bitcast(F32), ALU.subtract).then_inc(split, 1)

            lo_of_weights(wkvg_f, wkvg_hi, wkvg_lo, wkvg_hi_done, wkvg_split)
            lo_of_weights(wq_f, wq_hi, wq_lo, wq_hi_done, wq_split)
            inverse_deviation(3)
            normalise(3)
            inverse_deviation(4)
            normalise(4)
            split_wo()
            split_w1(0, 0, 1)
            split_w2(0, 0, 1)
            split_w1(1, 1, 1)
            split_w2(1, 1, 1)
            pool.wait_ge(l1_done, NBLK * KC)
            pool.wait_ge(l2_done, NBLK)
            split_w1(2, 0, 2)
            split_w2(2, 0, 2)
            for u in range(NBLK):
                gate_first(u)
            for u in range(NBLK, 2 * NBLK):
                accumulate(u, u)
                add_attention(u % NBLK)
            pool.wait_ge(l1_done, 2 * NBLK * KC)
            pool.wait_ge(l2_done, 2 * NBLK)
            split_w1(3, 1, 2)
            split_w2(3, 1, 2)
            pool.wait_ge(attn_added, NBLK)
            for u in range(2 * NBLK, 3 * NBLK):
                accumulate(u, u)
            with pool.Fori(2, PAIRS) as p:
                for par in range(2):
                    pool.wait_ge(l1_done, (2 * p + par - 1) * NBLK * KC)
                    pool.wait_ge(l2_done, (2 * p + par - 1) * NBLK)
                    split_w1(2 * p + par, par, p + 1)
                    split_w2(2 * p + par, par, p + 1)
                    for j in range(NBLK):
                        accumulate((2 * p + par - 1) * NBLK + j, j)
            for u in range(UNITS - NBLK, UNITS - 2):
                accumulate(u, u)
            for k in range(2):
                pool.wait_ge(fin_copied, k + 1)
                ts = slice(4 * k, 4 * k + 4)
                nc.gpsimd.tensor_tensor(res[:, ts, :], res[:, ts, :], x_tok[:, ts, :], ALU.add
                                        ).then_inc(res_pool_done, 1)

        def act_relu_and_hi(act, u, j, c, rounds):
            i = j % 2
            if j % NBLK == 0 and c == 0:
                act.wait_ge(b1_in[j // NBLK % 2], 16 * rounds)
            act.wait_ge(l1_done, u * KC + c + 1)
            nc.scalar.activation(h_ps[i][:, c, :], h_ps[i][:, c, :], ACT.Relu,
                                 bias=b1_f[j // NBLK % 2][:, c:c + 1]).then_inc(relu_done, 1)
            act.wait_ge(relu_done, u * KC + c + 1)
            if past(u, 2):
                act.wait_ge(l2_done, u - 1)
            nc.scalar.copy(h_hi[i][:, c, :], h_ps[i][:, c, :]).then_inc(hhi_done, 1)

        @block.scalar
        def _(act):
            act.wait_ge(eps_set, 1)
            nc.scalar.activation(warm[:, 0:1], eps[:], ACT.Sqrt).then_inc(warm_done, 1)

            def deviation(i):
                ts = slice(*PARTS[i])
                act.wait_ge(meanvar_done, PARTS[i][1])
                nc.scalar.activation(std[:, ts], mean_var[:, ts, 1], ACT.Sqrt, bias=eps[:, 0:1]).then_inc(std_done, 1)

            def normalise_tile(t):
                act.wait_ge(offset_done, t // 4 + 1)
                nc.scalar.activation(xn[:, t, :], x_tok[:, t, :], ACT.Identity, bias=offset[:, t:t + 1],
                                     scale=rstd[:, t:t + 1]).then_inc(xn_act_done, 1)

            def hi_of_weights(f, hi, arrived, hi_done):
                act.wait_ge(arrived, 16)
                nc.scalar.copy(hi[:], f[:]).then_inc(hi_done, 1)

            def hi_of_x(i):
                act.wait_ge(xT_done, i + 1)
                cols = x_hi[:, part_cols(i)]
                nc.scalar.copy(cols, xT_ps[i][:, 0:cols.shape[1]]).then_inc(xhi_done, 1)

            def exp_k_and_v(b):
                ts = slice(2 * b, 2 * b + 2)
                act.wait_ge(kvg_done, b + 1)
                nc.scalar.activation(kf[:, ts, :], kvg_ps[b % 2][:, :, 0:D], ACT.Relu, scale=-1.0
                                     ).then_inc(kneg_done, 1)
                nc.scalar.copy(vext[:, ts, 0:D], kvg_ps[b % 2][:, :, D:2 * D]).then_inc(v_done, 1)
                act.wait_ge(kneg_done, b + 1)
                nc.scalar.activation(kf[:, ts, :], kf[:, ts, :], ACT.Exp, scale=-1.0).then_inc(kexp_done, 1)

            def exp_q(k):
                act.wait_ge(q_done, k + 1)
                nc.scalar.activation(qf[:, blk_cols(k)], q_ps, ACT.Relu, scale=-1.0).then_inc(qneg_done, 1)
                act.wait_ge(qneg_done, k + 1)
                nc.scalar.activation(qf[:, blk_cols(k)], qf[:, blk_cols(k)], ACT.Exp, scale=-1.0
                                     ).then_inc(qexp_done, 1)

            def copy_att(k):
                act.wait_ge(attT_done, k + 1)
                nc.scalar.copy(attT_hi[:, blk_cols(k)], att_ps).then_inc(attT_hi_done, 1)

            def copy_attn(k):
                act.wait_ge(wo_done, k + 1)
                nc.scalar.copy(attn[:, blk_cols(k)], att_ps).then_inc(attn_copied, 1)

            def exp_of_logits():
                act.wait_ge(gate_step, 1)
                nc.scalar.activation(expd[:], shifted[:], ACT.Exp).then_inc(exp_done, 1)

            def copy_gates():
                act.wait_ge(gatesT_done, 1)
                nc.scalar.copy(gatesT[:], gatesT_ps).then_inc(gatesT_copied, 1)

            deviation(0)
            deviation(1)
            hi_of_weights(wkvg_f, wkvg_hi, wkvg_in, wkvg_hi_done)
            normalise_tile(3)
            hi_of_x(0)
            deviation(2)
            hi_of_x(1)
            hi_of_weights(wq_f, wq_hi, wq_in, wq_hi_done)
            nc.scalar.activation(warm[:, 1:2], eps[:], ACT.Exp).then_inc(warm_done, 1)
            normalise_tile(7)
            exp_k_and_v(0)
            hi_of_x(2)
            exp_k_and_v(1)
            exp_q(0)
            hi_of_x(3)
            exp_k_and_v(2)
            exp_k_and_v(3)
            exp_q(1)
            hi_of_x(4)
            exp_k_and_v(4)
            exp_k_and_v(5)
            exp_q(2)
            exp_k_and_v(6)
            exp_k_and_v(7)
            act_relu_and_hi(act, 0, 0, 0, 1)
            act_relu_and_hi(act, 0, 0, 1, 1)
            act_relu_and_hi(act, 1, 1, 0, 1)
            exp_of_logits()
            act_relu_and_hi(act, 1, 1, 1, 1)
            exp_q(3)
            copy_gates()
            act_relu_and_hi(act, 2, 2, 0, 1)
            act_relu_and_hi(act, 2, 2, 1, 1)
            act_relu_and_hi(act, 3, 3, 0, 1)
            act_relu_and_hi(act, 3, 3, 1, 1)
            copy_att(0)
            act_relu_and_hi(act, 4, 4, 0, 1)
            act_relu_and_hi(act, 4, 4, 1, 1)
            copy_attn(0)
            copy_att(1)
            act_relu_and_hi(act, 5, 5, 0, 1)
            act_relu_and_hi(act, 5, 5, 1, 1)
            copy_attn(1)
            copy_att(2)
            act_relu_and_hi(act, 6, 6, 0, 1)
            copy_attn(2)
            act_relu_and_hi(act, 6, 6, 1, 1)
            copy_att(3)
            act_relu_and_hi(act, 7, 7, 0, 1)
            act_relu_and_hi(act, 7, 7, 1, 1)
            copy_attn(3)
            with act.Fori(1, PAIRS) as p:
                for j in range(UPP):
                    for c in range(KC):
                        act_relu_and_hi(act, UPP * p + j, j, c, p + 1)
            for k in range(2):
                act.wait_ge(fin_done, k + 1)
                nc.scalar.copy(res[:, 4 * k:4 * k + 4, :], fin_ps[k].rearrange("p (t d) -> p t d", t=4)
                               ).then_inc(fin_copied, 1)
            for k in range(2):
                act.wait_ge(res_pool_done, k + 1)
                act.dma_start(out_view[:, 2 * k:2 * k + 2],
                              res[:, 4 * k:4 * k + 4, :].rearrange("p (b r) d -> p b r d", r=R)
                              ).then_inc(out_written, 16)

        @block.vector
        def _(dve):
            def statistics(i):
                dve.wait_ge(x_in[i], 16)
                for t in range(*PARTS[i]):
                    nc.vector.bn_stats(stats[:, t, :], x_tok[:, t, :]).then_inc(stats_done, 1)
                for t in range(*PARTS[i]):
                    dve.wait_ge(stats_done, t + 1)
                    nc.vector.bn_aggr(mean_var[:, t, :], stats[:, t, :]).then_inc(meanvar_done, 1)

            def mask_kv(k):
                dve.wait_ge(kv_done, k + 1)
                if k == 0:
                    dve.wait_ge(consts_in, 16)
                nc.vector.tensor_tensor(kv[:, 2 * k:2 * k + 2, :],
                                        att_ps.rearrange("p (b n) -> p b n", b=2)[:, :, 0:NV],
                                        kv_mask.unsqueeze(1).to_broadcast([P, 2, NV]), ALU.mult
                                        ).then_inc(kvmask_done, 1)

            def lo_of_x(i):
                dve.wait_ge(xhi_done, i + 1)
                cols = x_lo[:, part_cols(i)]
                nc.vector.tensor_tensor(cols, xT_ps[i][:, 0:cols.shape[1]], x_hi[:, part_cols(i)].bitcast(F32),
                                        ALU.subtract).then_inc(xlo_done, 1)

            def finish_k(b):
                ts = slice(2 * b, 2 * b + 2)
                dve.wait_ge(kexp_done, b + 1)
                dve.wait_ge(v_done, b + 1)
                if b == 0:
                    dve.wait_ge(gate_b_in, 16)
                nc.vector.tensor_tensor(logits[:, ts, :], kvg_ps[b % 2][:, :, 2 * D:KVG],
                                        gate_bias[:].unsqueeze(1).to_broadcast([P, 2, E]), ALU.add
                                        ).then_inc(logits_done, 1)
                nc.vector.scalar_tensor_tensor(out=kf[:, ts, :], in0=kvg_ps[b % 2][:, :, 0:D], scalar=0.0,
                                               in1=kf[:, ts, :], op0=ALU.max, op1=ALU.add
                                               ).then_inc(kf_done, 1)

            def top_two(b):
                dve.wait_ge(logits_done, b + 1)
                for t in (2 * b, 2 * b + 1):
                    nc.vector.max(top8[:, t, :], logits[:, t, :]).then_inc(top_done, 1)
                for t in (2 * b, 2 * b + 1):
                    dve.wait_ge(top_done, t + 1)
                    nc.vector.max_index(idx8[:, t, :], top8[:, t, :], logits[:, t, :]).then_inc(idx_done, 1)

            def finish_q(k):
                dve.wait_ge(qexp_done, k + 1)
                nc.vector.scalar_tensor_tensor(out=qf[:, blk_cols(k)], in0=q_ps, scalar=0.0,
                                               in1=qf[:, blk_cols(k)], op0=ALU.max, op1=ALU.add
                                               ).then_inc(qf_done, 1)

            def inverse_deviation(i):
                ts = slice(*PARTS[i])
                dve.wait_ge(std_done, i + 1)
                nc.vector.reciprocal(rstd[:, ts], std[:, ts]).then_inc(rstd_done, 1)

            def offsets(i):
                ts = slice(*PARTS[i])
                dve.wait_ge(rstd_done, i + 1)
                nc.vector.scalar_tensor_tensor(out=offset[:, ts], in0=mean_var[:, ts, 0], scalar=-1.0, in1=rstd[:, ts],
                                               op0=ALU.mult, op1=ALU.mult).then_inc(offset_done, 1)

            def normalise(t):
                dve.wait_ge(rstd_done, sum(t >= a for a, _ in PARTS))
                nc.vector.tensor_scalar(xn[:, t, :], x_tok[:, t, :], mean_var[:, t, 0:1], rstd[:, t:t + 1],
                                        ALU.subtract, ALU.mult).then_inc(xn_done, 1)

            def shift_logits():
                dve.wait_ge(top_done, T)
                nc.vector.tensor_tensor(shifted[:], logits[:], top8[:, :, 0:1].to_broadcast([P, T, E]),
                                        ALU.subtract).then_inc(gate_step, 1)

            def pick_experts():
                dve.wait_ge(idx_done, T)
                nc.vector.tensor_copy(idxf[:, :, 0:TOP], idx8[:, :, 0:TOP]).then_inc(pick_step, 1)
                all_ramp = ramp.unsqueeze(1).to_broadcast([P, T, E])
                dve.wait_ge(pick_step, 1)
                nc.vector.tensor_tensor(is_first[:], all_ramp, idxf[:, :, 0:1].to_broadcast([P, T, E]),
                                        ALU.is_equal).then_inc(pick_step, 1)
                nc.vector.tensor_tensor(is_second[:], all_ramp, idxf[:, :, 1:2].to_broadcast([P, T, E]),
                                        ALU.is_equal).then_inc(pick_step, 1)
                dve.wait_ge(pick_step, 3)
                nc.vector.tensor_tensor(picked[:], is_first[:], is_second[:], ALU.add).then_inc(pick_step, 1)

            def gate_values():
                dve.wait_ge(exp_done, 1)
                nc.vector.reduce_sum(expsum[:], expd[:], AX_X).then_inc(gate_step, 1)
                dve.wait_ge(pick_step, 4)
                nc.vector.tensor_tensor(picked[:], expd[:], picked[:], ALU.mult).then_inc(gate_step, 1)
                dve.wait_ge(gate_step, 2)
                nc.vector.reciprocal(rexpsum[:], expsum[:]).then_inc(gate_step, 1)
                dve.wait_ge(gate_step, 4)
                nc.vector.tensor_tensor(gates[:].rearrange("p e t -> p t e"), picked[:],
                                        rexpsum[:].unsqueeze(2).to_broadcast([P, T, E]), ALU.mult
                                        ).then_inc(gates_done, 1)

            def divide(b):
                ts = slice(2 * b, 2 * b + 2)
                both = num_ps[:, 0:2 * NV].rearrange("p (r n) -> p r n", r=2)
                dve.wait_ge(num_done, b + 1)
                nc.vector.tensor_scalar(den[:, ts, :], both[:, :, D:NV], DEN_EPS, None, ALU.add
                                        ).then_inc(den_done, 1)
                dve.wait_ge(den_done, b + 1)
                nc.vector.reciprocal(rden[:, ts, :], den[:, ts, :]).then_inc(rden_done, 1)
                dve.wait_ge(rden_done, b + 1)
                nc.vector.tensor_tensor(
                    att[:, ts, :].rearrange("p r (h d) -> p r h d", h=HEADS),
                    both[:, :, 0:D].rearrange("p r (h d) -> p r h d", h=HEADS),
                    rden[:, ts, :].unsqueeze(3).to_broadcast([P, R, HEADS, D // HEADS]), ALU.mult
                    ).then_inc(att_done, 1)

            def lo_of_att(k):
                dve.wait_ge(attT_hi_done, k + 1)
                nc.vector.tensor_tensor(attT_lo[:, blk_cols(k)], att_ps, attT_hi[:, blk_cols(k)].bitcast(F32),
                                        ALU.subtract).then_inc(attT_lo_done, 1)

            def lo_of_h(u, j, c):
                i = j % 2
                dve.wait_ge(hhi_done, u * KC + c + 1)
                nc.vector.tensor_tensor(h_lo[i][:, c, :], h_ps[i][:, c, :], h_hi[i][:, c, :].bitcast(F32),
                                        ALU.subtract).then_inc(hlo_done, 1)

            def gate_output(u, j, e, rounds):
                blk = j % NBLK
                par = j // NBLK % 2
                dve.wait_ge(l2_done, u + 1)
                if blk == 0:
                    dve.wait_ge(gate_row_in[par], rounds * 16)
                if past(u, 2 * NBLK):
                    dve.wait_ge(acc_done, u - NBLK + 1)
                nc.vector.scalar_tensor_tensor(out=y[j % 4][:], in0=y_ps[j % 2], scalar=b2_f[:, bass.ds(e, 1)],
                                               in1=gate_row[par][:, blk_cols(blk)], op0=ALU.add, op1=ALU.mult
                                               ).then_inc(gated_done, 1)

            def first_output(u):
                dve.wait_ge(l2_done, u + 1)
                if u == 0:
                    dve.wait_ge(b2_in, 16)
                nc.vector.tensor_scalar(acc[:, blk_cols(u)], y_ps[u % 2], b2_f[:, 0:1], None, ALU.add
                                        ).then_inc(gated_done, 1)

            statistics(0)
            statistics(1)
            inverse_deviation(0)
            normalise(0)
            inverse_deviation(1)
            normalise(1)
            offsets(1)
            normalise(2)
            statistics(2)
            statistics(3)
            inverse_deviation(2)
            lo_of_x(0)
            normalise(4)
            offsets(2)
            normalise(5)
            normalise(6)
            lo_of_x(1)
            statistics(4)
            lo_of_x(2)
            finish_k(0)
            top_two(0)
            finish_k(1)
            finish_q(0)
            lo_of_x(3)
            top_two(1)
            finish_k(2)
            top_two(2)
            finish_k(3)
            mask_kv(0)
            finish_q(1)
            lo_of_x(4)
            top_two(3)
            finish_k(4)
            top_two(4)
            finish_k(5)
            top_two(5)
            finish_q(2)
            mask_kv(1)
            finish_k(6)
            top_two(6)
            finish_k(7)
            top_two(7)
            pick_experts()
            lo_of_h(0, 0, 0)
            shift_logits()
            lo_of_h(0, 0, 1)
            mask_kv(2)
            gate_values()
            first_output(0)
            lo_of_h(1, 1, 0)
            mask_kv(3)
            finish_q(3)
            lo_of_h(1, 1, 1)
            divide(0)
            lo_of_h(2, 2, 0)
            lo_of_h(2, 2, 1)
            divide(1)
            lo_of_h(3, 3, 0)
            lo_of_h(3, 3, 1)
            divide(2)
            lo_of_att(0)
            first_output(1)
            divide(3)
            first_output(2)
            divide(4)
            lo_of_att(1)
            lo_of_h(4, 4, 0)
            lo_of_h(4, 4, 1)
            divide(5)
            lo_of_h(5, 5, 0)
            lo_of_h(5, 5, 1)
            divide(6)
            lo_of_att(2)
            first_output(3)
            gate_output(4, 4, 1, 1)
            divide(7)
            lo_of_h(6, 6, 0)
            lo_of_h(6, 6, 1)
            lo_of_att(3)
            gate_output(5, 5, 1, 1)
            gate_output(6, 6, 1, 1)
            lo_of_h(7, 7, 0)
            lo_of_h(7, 7, 1)
            with dve.Fori(1, PAIRS) as p:
                for j in range(UPP):
                    for c in range(KC):
                        lo_of_h(UPP * p + j, j, c)
                    if j == 0:
                        gate_output(UPP * p - 1, UPP - 1, 2 * p - 1, p)
                    else:
                        gate_output(UPP * p + (j - 1), j - 1, 2 * p + (j - 1) // NBLK, p + 1)

            def accumulate_last_but_one(u):
                dve.wait_ge(gated_done, u + 1)
                dve.wait_ge(acc_done, u - NBLK + 1)
                cols = acc[:, blk_cols(u % NBLK)]
                nc.vector.tensor_tensor(cols, cols, y[u % 4][:], ALU.add).then_inc(last_but_one_acc_done, 1)

            def finish(k):
                dve.wait_ge(fin_done, k + 1)
                nc.vector.tensor_tensor(res[:, 4 * k:4 * k + 4, :],
                                        fin_ps[k].rearrange("p (t d) -> p t d", t=4),
                                        x_tok[:, 4 * k:4 * k + 4, :], ALU.add).then_inc(res_done, 1)

            accumulate_last_but_one(UNITS - 2)
            gate_output(UNITS - 1, UPP - 1, E - 1, PAIRS)
            finish(2)
            finish(3)

        @block.tensor
        def _(pe):
            def three(out_ap, lhs_hi, lhs_lo, rhs_hi, rhs_lo, start=True, stop=True):
                nc.tensor.matmul(out_ap, lhs_hi, rhs_hi, start=start, stop=False)
                nc.tensor.matmul(out_ap, lhs_hi, rhs_lo, start=False, stop=False)
                return nc.tensor.matmul(out_ap, lhs_lo, rhs_hi, start=False, stop=stop)

            def transpose_x(i):
                if i == 0:
                    pe.wait_ge(consts_in, 16)
                    pe.wait_ge(xn_done, 2)
                elif i == 1:
                    pe.wait_ge(xn_done, 3)
                    pe.wait_ge(xn_act_done, 1)
                elif i == 2:
                    pe.wait_ge(xn_done, 6)
                    pe.wait_ge(xn_act_done, 2)
                else:
                    pe.wait_ge(xn_pool_done, i - 2)
                if i == 3:
                    pe.wait_ge(xlo_done, 1)
                elif i == 4:
                    pe.wait_ge(xlo_done, 3)
                first, end = PARTS[i]
                for t in range(first, end):
                    last = nc.tensor.transpose(xT_ps[i][:, (t - first) * P:(t - first + 1) * P], xn[:, t, :], ident)
                last.then_inc(xT_done, 1)

            def project_kvg(b):
                if b == 0:
                    pe.wait_ge(wkvg_split, 1)
                pe.wait_ge(xlo_done, sum(R * b >= a for a, _ in PARTS))
                if b >= 2:
                    pe.wait_ge(kf_done, b - 1)
                for r in range(2):
                    cols = slice((2 * b + r) * P, (2 * b + r + 1) * P)
                    last = three(kvg_ps[b % 2][:, r, 0:KVG], x_hi[:, cols], x_lo[:, cols], wkvg_hi[:], wkvg_lo[:])
                last.then_inc(kvg_done, 1)

            def project_q(k):
                if k == 0:
                    pe.wait_ge(wq_split, 1)
                else:
                    pe.wait_ge(qf_done, k)
                pe.wait_ge(xlo_done, sum(4 * k + 3 >= a for a, _ in PARTS))
                three(q_ps, wq_hi[:], wq_lo[:], x_hi[:, blk_cols(k)], x_lo[:, blk_cols(k)]).then_inc(q_done, 1)

            def keys_values(k):
                pe.wait_ge(kf_done, 2 * k + 2)
                if k == 0:
                    pe.wait_ge(ones_set, 3)
                else:
                    pe.wait_ge(kvmask_done, k)
                for b in range(2):
                    for r in range(2):
                        t = 4 * k + 2 * b + r
                        last = nc.tensor.matmul(att_ps[:, 256 * b:256 * b + NV], kf[:, t, :], vext[:, t, :],
                                                start=(r == 0), stop=(r == 1))
                last.then_inc(kv_done, 1)

            def numerator(b):
                pe.wait_ge(kvmask_done, b // 2 + 1)
                if b == 0:
                    pe.wait_ge(qf_done, NBLK)
                else:
                    pe.wait_ge(att_done, b)
                for r in range(2):
                    t = 2 * b + r
                    last = nc.tensor.matmul(num_ps[:, r * NV:(r + 1) * NV], qf[:, t * P:(t + 1) * P], kv[:, b, :],
                                            start=True, stop=True)
                last.then_inc(num_done, 1)

            def transpose_att(k):
                pe.wait_ge(att_done, 2 * k + 2)
                if k == 0:
                    pe.wait_ge(kvmask_done, NBLK)
                else:
                    pe.wait_ge(attn_copied, k)
                for t in range(4):
                    last = nc.tensor.transpose(att_ps[:, t * P:(t + 1) * P], att[:, 4 * k + t, :], ident)
                last.then_inc(attT_done, 1)

            def project_out(k):
                if k == 0:
                    pe.wait_ge(wo_split, 1)
                pe.wait_ge(attT_lo_done, k + 1)
                three(att_ps, wo_hi[:], wo_lo[:], attT_hi[:, blk_cols(k)], attT_lo[:, blk_cols(k)]).then_inc(wo_done, 1)

            def first_product(u, j, e, c):
                par, blk, i = j // NBLK % 2, j % NBLK, j % 2
                if blk == 0 and c == 0:
                    pe.wait_ge(w1_split, e + 1)
                if past(u, 2):
                    pe.wait_ge(hlo_done, (u - 2) * KC + c + 1)
                elif u == 0:
                    pe.wait_ge(xlo_done, len(PARTS))
                else:
                    pe.wait_ge(kf_done, B - 1)
                w = slice(c * P, (c + 1) * P)
                three(h_ps[i][:, c, :], w1_hi[par][:, w], w1_lo[par][:, w],
                      x_hi[:, blk_cols(blk)], x_lo[:, blk_cols(blk)]).then_inc(l1_done, 1)

            def second_product(u, j, e, c):
                par, blk, i = j // NBLK % 2, j % NBLK, j % 2
                if blk == 0 and c == 0:
                    pe.wait_ge(w2_split, e + 1)
                if c == 0 and past(u, 2):
                    pe.wait_ge(gated_done, u - 1)
                elif c == 0 and u == 0:
                    pe.wait_ge(kf_done, B)
                elif c == 0:
                    pe.wait_ge(gatesT_copied, 1)
                w = slice(c * D, (c + 1) * D)
                pe.wait_ge(hlo_done, u * KC + c + 1)
                last = three(y_ps[i], w2_hi[par][:, w], w2_lo[par][:, w], h_hi[i][:, c, :], h_lo[i][:, c, :],
                             start=(c == 0), stop=(c == KC - 1))
                if c == KC - 1:
                    last.then_inc(l2_done, 1)

            def warm_up(times):
                pe.wait_ge(ones_set, 1)
                for _ in range(times):
                    last = nc.tensor.matmul(att_ps[:, 0:P], ones[:, 0:P], ones[:, 0:P], start=True, stop=True)
                last.then_inc(pe_warm, 1)

            def transpose_gates():
                pe.wait_ge(gates_done, 1)
                pe.wait_ge(kf_done, B)
                nc.tensor.transpose(gatesT_ps, gates[:].rearrange("p e t -> p (e t)"), ident).then_inc(gatesT_done, 1)

            warm_up(WARM_UPS_BEFORE)
            transpose_x(0)
            transpose_x(1)
            warm_up(WARM_UPS_AFTER)
            project_kvg(0)
            transpose_x(2)
            project_kvg(1)
            project_q(0)
            transpose_x(3)
            project_kvg(2)
            project_kvg(3)
            project_q(1)
            keys_values(0)
            transpose_x(4)
            project_kvg(4)
            project_kvg(5)
            project_q(2)
            keys_values(1)
            project_kvg(6)
            project_kvg(7)
            first_product(0, 0, 0, 0)
            project_q(3)
            first_product(0, 0, 0, 1)
            first_product(1, 1, 0, 0)
            first_product(1, 1, 0, 1)
            keys_values(2)
            second_product(0, 0, 0, 0)
            second_product(0, 0, 0, 1)
            keys_values(3)
            transpose_gates()
            first_product(2, 2, 0, 0)
            first_product(2, 2, 0, 1)
            second_product(1, 1, 0, 0)
            numerator(0)
            second_product(1, 1, 0, 1)
            first_product(3, 3, 0, 0)
            first_product(3, 3, 0, 1)
            numerator(1)
            second_product(2, 2, 0, 0)
            second_product(2, 2, 0, 1)
            transpose_att(0)
            numerator(2)
            first_product(4, 4, 1, 0)
            first_product(4, 4, 1, 1)
            first_product(5, 5, 1, 0)
            numerator(3)
            project_out(0)
            second_product(3, 3, 0, 0)
            numerator(4)
            transpose_att(1)
            second_product(3, 3, 0, 1)
            first_product(5, 5, 1, 1)
            numerator(5)
            project_out(1)
            second_product(4, 4, 1, 0)
            second_product(4, 4, 1, 1)
            numerator(6)
            transpose_att(2)
            first_product(6, 6, 1, 0)
            first_product(6, 6, 1, 1)
            first_product(7, 7, 1, 0)
            project_out(2)
            numerator(7)
            first_product(7, 7, 1, 1)
            second_product(5, 5, 1, 0)
            transpose_att(3)
            second_product(5, 5, 1, 1)
            second_product(6, 6, 1, 0)
            second_product(6, 6, 1, 1)
            project_out(3)
            with pe.Fori(1, PAIRS) as p:
                for j in range(UPP):
                    for c in range(KC):
                        first_product(UPP * p + j, j, 2 * p + j // NBLK, c)
                    for c in range(KC):
                        if j == 0:
                            second_product(UPP * p - 1, UPP - 1, 2 * p - 1, c)
                        else:
                            second_product(UPP * p + (j - 1), j - 1, 2 * p + (j - 1) // NBLK, c)

            def turn_back(k):
                if k < 2:
                    pe.wait_ge(acc_done, UNITS - NBLK + k + 1)
                else:
                    pe.wait_ge(last_but_one_acc_done, 1)
                for t in range(4):
                    last = nc.tensor.transpose(fin_ps[k][:, t * P:(t + 1) * P],
                                               acc[:, (4 * k + t) * P:(4 * k + t + 1) * P], ident)
                last.then_inc(fin_done, 1)

            def turn_back_last(source, start):
                for t in range(4):
                    last = nc.tensor.matmul(fin_ps[3][:, t * P:(t + 1) * P], source[:, t * P:(t + 1) * P], ident,
                                            start=start and t == 0, stop=not start and t == 3)
                return last

            turn_back(0)
            second_product(UNITS - 1, UPP - 1, E - 1, 0)
            turn_back(1)
            second_product(UNITS - 1, UPP - 1, E - 1, 1)
            pe.wait_ge(acc_done, UNITS - NBLK)
            turn_back_last(acc[:, blk_cols(NBLK - 1)], True)
            turn_back(2)
            pe.wait_ge(gated_done, UNITS)
            turn_back_last(y[(UNITS - 1) % 4][:], False).then_inc(fin_done, 1)


def kernel(L0_attn_x, L0_attn_Wq, L0_attn_Wk, L0_attn_Wv, L0_attn_Wo, L0_ffn_gate_w, L0_ffn_gate_b,
           L0_ffn_w1, L0_ffn_b1, L0_ffn_w2, L0_ffn_b2):
    import concourse.bacc as bacc
    from concourse.bass_utils import run_bass_kernel_spmd

    x = np.ascontiguousarray(L0_attn_x)
    E, D, H = L0_ffn_w1.shape
    T = x.shape[0] * x.shape[1] // P
    arrays = {
        "x": x,
        "wkvg": np.ascontiguousarray(np.concatenate(
            [np.asarray(L0_attn_Wk), np.asarray(L0_attn_Wv), np.asarray(L0_ffn_gate_w).T], axis=1)),
        "wq": np.ascontiguousarray(L0_attn_Wq),
        "wo": np.ascontiguousarray(L0_attn_Wo),
        "gate_b": np.ascontiguousarray(L0_ffn_gate_b),
        "w1": np.ascontiguousarray(L0_ffn_w1),
        "b1": np.ascontiguousarray(np.asarray(L0_ffn_b1).reshape(E, H // P, P).transpose(0, 2, 1)).reshape(E * P, H // P),
        "w2": np.ascontiguousarray(L0_ffn_w2),
        "b2": np.ascontiguousarray(np.asarray(L0_ffn_b2).T),
        "consts": shape_constants(D),
    }
    nc = bacc.Bacc("TRN2", target_bir_lowering=False, num_devices=1)
    args = [nc.dram_tensor(f"in_{n}", a.shape, mybir.dt.from_np(a.dtype), kind="ExternalInput").ap()
            for n, a in arrays.items()]
    gates_dram = nc.dram_tensor("gates_dram", (E * T, P), F32, kind="Internal").ap()
    out = nc.dram_tensor("out", x.shape, F32, kind="ExternalOutput").ap()
    linear_attention_with_top2_experts(nc, *args, gates_dram, out)
    r = run_bass_kernel_spmd(nc, [{f"in_{n}": a for n, a in arrays.items()}], core_ids=[0])
    return np.asarray(r.results[0]["out"])
```
